# Optimizing a Trainium2 kernel written in Bass

```python
import numpy as np
import jax
import jax.numpy as jnp

def _softmax(x, axis=-1):
    return jax.nn.softmax(x, axis=axis)

def _gelu(x):
    return jax.nn.gelu(x, approximate=True)

def _silu(x):
    return jax.nn.silu(x)

def _sigmoid(x):
    return jax.nn.sigmoid(x)

def _layernorm(x, axis=-1, eps=1e-05):
    m = jnp.mean(x, axis=axis, keepdims=True)
    v = jnp.var(x, axis=axis, keepdims=True)
    return (x - m) / jnp.sqrt(v + eps)

def _scatter_add(tgt, idx, src, axis=0):
    return tgt.at[idx].add(src)

def _segment_sum(src, seg, n):
    return jax.ops.segment_sum(src, seg, n)
kernel_name = 'mk_macaron_d1_jaxref_r8_94b707'

def setup_inputs(seed: int=0):
    np.random.seed(seed)
    _w = jnp.asarray

    def _L0_attn_setup():
        import jax, jax.numpy as jnp
        import numpy as np
        EPS = 1e-08
        key = jax.random.key(seed)
        x = jax.random.normal(key, (32, 200, 128), dtype=jnp.float32)
        return {'x': x}
    _L0_attn_in = _L0_attn_setup()

    def _L0_ffn_setup():
        import jax, jax.numpy as jnp
        import numpy as np
        D_MODEL = 128
        N_HEADS = 16
        HEAD_DIM = D_MODEL // N_HEADS
        KV_LATENT = 64
        N_EXPERTS = 4
        D_HIDDEN = 4 * D_MODEL
        B, T = (2, 128)

        def rmsnorm(x, w, eps=1e-06):
            return w * (x * jax.lax.rsqrt(jnp.mean(x * x, axis=-1, keepdims=True) + eps))

        def layernorm(x, g, b, eps=1e-05):
            mu = jnp.mean(x, axis=-1, keepdims=True)
            var = jnp.mean((x - mu) ** 2, axis=-1, keepdims=True)
            return (x - mu) * jax.lax.rsqrt(var + eps) * g + b

        def apply_rope(x):
            t, d = (x.shape[2], x.shape[3])
            half = d // 2
            pos = jnp.arange(t, dtype=x.dtype)[:, None]
            inv_freq = 1.0 / 10000.0 ** (jnp.arange(half, dtype=x.dtype) / half)
            ang = pos * inv_freq[None, :]
            sin, cos = (jnp.sin(ang), jnp.cos(ang))
            x1, x2 = (x[..., :half], x[..., half:])
            return jnp.concatenate([x1 * cos - x2 * sin, x1 * sin + x2 * cos], axis=-1)

        def mla_attention(x, Wq, Wdkv, Wuk, Wuv, Wo, ln_g, ln_b):
            b, t, _ = x.shape
            q = (x @ Wq.T).reshape(b, t, N_HEADS, HEAD_DIM).transpose(0, 2, 1, 3)
            latent = layernorm(x @ Wdkv.T, ln_g, ln_b)
            k = (latent @ Wuk.T).reshape(b, t, N_HEADS, HEAD_DIM).transpose(0, 2, 1, 3)
            v = (latent @ Wuv.T).reshape(b, t, N_HEADS, HEAD_DIM).transpose(0, 2, 1, 3)
            q = apply_rope(q)
            k = apply_rope(k)
            scores = jnp.einsum('bhqd,bhkd->bhqk', q, k) / np.sqrt(HEAD_DIM)
            causal = jnp.tril(jnp.ones((t, t), dtype=bool))
            scores = jnp.where(causal, scores, -jnp.inf)
            attn = jax.nn.softmax(scores, axis=-1)
            out = jnp.einsum('bhqk,bhkd->bhqd', attn, v).transpose(0, 2, 1, 3).reshape(b, t, D_MODEL)
            return out @ Wo.T

        def moe(x, gate_w, gate_b, W1, b1, W2, b2):
            logits = x @ gate_w.T + gate_b
            top = jnp.argmax(logits, axis=-1)
            onehot = jax.nn.one_hot(top, N_EXPERTS, dtype=x.dtype)
            h = jax.nn.relu(jnp.einsum('btd,ehd->bteh', x, W1) + b1)
            y = jnp.einsum('bteh,edh->bted', h, W2) + b2
            return jnp.einsum('bted,bte->btd', y, onehot)
        key = jax.random.key(seed)
        ks = jax.random.split(key, 16)
        s = lambda fan_in: 1.0 / np.sqrt(fan_in)
        return {'x': jax.random.normal(ks[0], (B, T, D_MODEL), jnp.float32), 'norm1_w': jnp.ones((D_MODEL,), jnp.float32), 'norm2_w': jnp.ones((D_MODEL,), jnp.float32), 'Wq': jax.random.normal(ks[1], (D_MODEL, D_MODEL), jnp.float32) * s(D_MODEL), 'Wdkv': jax.random.normal(ks[2], (KV_LATENT, D_MODEL), jnp.float32) * s(D_MODEL), 'Wuk': jax.random.normal(ks[3], (D_MODEL, KV_LATENT), jnp.float32) * s(KV_LATENT), 'Wuv': jax.random.normal(ks[4], (D_MODEL, KV_LATENT), jnp.float32) * s(KV_LATENT), 'Wo': jax.random.normal(ks[5], (D_MODEL, D_MODEL), jnp.float32) * s(D_MODEL), 'ln_g': jnp.ones((KV_LATENT,), jnp.float32), 'ln_b': jnp.zeros((KV_LATENT,), jnp.float32), 'gate_w': jax.random.normal(ks[6], (N_EXPERTS, D_MODEL), jnp.float32) * s(D_MODEL), 'gate_b': jnp.zeros((N_EXPERTS,), jnp.float32), 'W1': jax.random.normal(ks[7], (N_EXPERTS, D_HIDDEN, D_MODEL), jnp.float32) * s(D_MODEL), 'b1': jnp.zeros((N_EXPERTS, D_HIDDEN), jnp.float32), 'W2': jax.random.normal(ks[8], (N_EXPERTS, D_MODEL, D_HIDDEN), jnp.float32) * s(D_HIDDEN), 'b2': jnp.zeros((N_EXPERTS, D_MODEL), jnp.float32)}
    _L0_ffn_in = _L0_ffn_setup()
    _d = {'L0_attn_x': _L0_attn_in['x'], 'L0_ffn_norm1_w': _L0_ffn_in['norm1_w'], 'L0_ffn_norm2_w': _L0_ffn_in['norm2_w'], 'L0_ffn_Wq': _L0_ffn_in['Wq'], 'L0_ffn_Wdkv': _L0_ffn_in['Wdkv'], 'L0_ffn_Wuk': _L0_ffn_in['Wuk'], 'L0_ffn_Wuv': _L0_ffn_in['Wuv'], 'L0_ffn_Wo': _L0_ffn_in['Wo'], 'L0_ffn_ln_g': _L0_ffn_in['ln_g'], 'L0_ffn_ln_b': _L0_ffn_in['ln_b'], 'L0_ffn_gate_w': _L0_ffn_in['gate_w'], 'L0_ffn_gate_b': _L0_ffn_in['gate_b'], 'L0_ffn_W1': _L0_ffn_in['W1'], 'L0_ffn_b1': _L0_ffn_in['b1'], 'L0_ffn_W2': _L0_ffn_in['W2'], 'L0_ffn_b2': _L0_ffn_in['b2']}
    _x0 = _d['L0_attn_x']
    _d['L0_attn_x'] = jax.random.normal(jax.random.fold_in(jax.random.key(seed), 1), (4, 512, 128), dtype=_x0.dtype)
    del _x0
    return _d

def reference(L0_attn_x, L0_ffn_norm1_w, L0_ffn_norm2_w, L0_ffn_Wq, L0_ffn_Wdkv, L0_ffn_Wuk, L0_ffn_Wuv, L0_ffn_Wo, L0_ffn_ln_g, L0_ffn_ln_b, L0_ffn_gate_w, L0_ffn_gate_b, L0_ffn_W1, L0_ffn_b1, L0_ffn_W2, L0_ffn_b2):

    def _L0_attn_ref(x):
        import jax, jax.numpy as jnp
        import numpy as np
        EPS = 1e-08
        norms = jnp.linalg.norm(x, axis=-1)
        dots = jnp.einsum('bil,bjl->bij', x, x)
        sim = dots / jnp.maximum(norms[:, :, None] * norms[:, None, :], EPS)
        atten = jax.nn.softmax(sim, axis=-1)
        out = jnp.einsum('bij,bjl->bil', atten, x) + x
        return out

    def _L0_ffn_ref(x, norm1_w, norm2_w, Wq, Wdkv, Wuk, Wuv, Wo, ln_g, ln_b, gate_w, gate_b, W1, b1, W2, b2):
        import jax, jax.numpy as jnp
        import numpy as np
        D_MODEL = 128
        N_HEADS = 16
        HEAD_DIM = D_MODEL // N_HEADS
        KV_LATENT = 64
        N_EXPERTS = 4
        D_HIDDEN = 4 * D_MODEL
        B, T = (2, 128)

        def rmsnorm(x, w, eps=1e-06):
            return w * (x * jax.lax.rsqrt(jnp.mean(x * x, axis=-1, keepdims=True) + eps))

        def layernorm(x, g, b, eps=1e-05):
            mu = jnp.mean(x, axis=-1, keepdims=True)
            var = jnp.mean((x - mu) ** 2, axis=-1, keepdims=True)
            return (x - mu) * jax.lax.rsqrt(var + eps) * g + b

        def apply_rope(x):
            t, d = (x.shape[2], x.shape[3])
            half = d // 2
            pos = jnp.arange(t, dtype=x.dtype)[:, None]
            inv_freq = 1.0 / 10000.0 ** (jnp.arange(half, dtype=x.dtype) / half)
            ang = pos * inv_freq[None, :]
            sin, cos = (jnp.sin(ang), jnp.cos(ang))
            x1, x2 = (x[..., :half], x[..., half:])
            return jnp.concatenate([x1 * cos - x2 * sin, x1 * sin + x2 * cos], axis=-1)

        def mla_attention(x, Wq, Wdkv, Wuk, Wuv, Wo, ln_g, ln_b):
            b, t, _ = x.shape
            q = (x @ Wq.T).reshape(b, t, N_HEADS, HEAD_DIM).transpose(0, 2, 1, 3)
            latent = layernorm(x @ Wdkv.T, ln_g, ln_b)
            k = (latent @ Wuk.T).reshape(b, t, N_HEADS, HEAD_DIM).transpose(0, 2, 1, 3)
            v = (latent @ Wuv.T).reshape(b, t, N_HEADS, HEAD_DIM).transpose(0, 2, 1, 3)
            q = apply_rope(q)
            k = apply_rope(k)
            scores = jnp.einsum('bhqd,bhkd->bhqk', q, k) / np.sqrt(HEAD_DIM)
            causal = jnp.tril(jnp.ones((t, t), dtype=bool))
            scores = jnp.where(causal, scores, -jnp.inf)
            attn = jax.nn.softmax(scores, axis=-1)
            out = jnp.einsum('bhqk,bhkd->bhqd', attn, v).transpose(0, 2, 1, 3).reshape(b, t, D_MODEL)
            return out @ Wo.T

        def moe(x, gate_w, gate_b, W1, b1, W2, b2):
            logits = x @ gate_w.T + gate_b
            top = jnp.argmax(logits, axis=-1)
            onehot = jax.nn.one_hot(top, N_EXPERTS, dtype=x.dtype)
            h = jax.nn.relu(jnp.einsum('btd,ehd->bteh', x, W1) + b1)
            y = jnp.einsum('bteh,edh->bted', h, W2) + b2
            return jnp.einsum('bted,bte->btd', y, onehot)
        x = x + mla_attention(rmsnorm(x, norm1_w), Wq, Wdkv, Wuk, Wuv, Wo, ln_g, ln_b)
        x = x + moe(rmsnorm(x, norm2_w), gate_w, gate_b, W1, b1, W2, b2)
        return x
    x = L0_attn_x
    x = x + 0.5 * _L0_ffn_ref(_layernorm(x, axis=-1), L0_ffn_norm1_w, L0_ffn_norm2_w, L0_ffn_Wq, L0_ffn_Wdkv, L0_ffn_Wuk, L0_ffn_Wuv, L0_ffn_Wo, L0_ffn_ln_g, L0_ffn_ln_b, L0_ffn_gate_w, L0_ffn_gate_b, L0_ffn_W1, L0_ffn_b1, L0_ffn_W2, L0_ffn_b2)
    x = x + _L0_attn_ref(_layernorm(x, axis=-1))
    x = x + 0.5 * _L0_ffn_ref(_layernorm(x, axis=-1), L0_ffn_norm1_w, L0_ffn_norm2_w, L0_ffn_Wq, L0_ffn_Wdkv, L0_ffn_Wuk, L0_ffn_Wuv, L0_ffn_Wo, L0_ffn_ln_g, L0_ffn_ln_b, L0_ffn_gate_w, L0_ffn_gate_b, L0_ffn_W1, L0_ffn_b1, L0_ffn_W2, L0_ffn_b2)
    return x

_drawn_inputs = setup_inputs


def setup_inputs(seed=0):
    import zlib

    import numpy as np

    out = dict(_drawn_inputs(seed))
    spreads = {'L0_ffn_norm1_w': (1.0, 0.2),
     'L0_ffn_norm2_w': (1.0, 0.2),
     'L0_ffn_ln_g': (1.0, 0.2),
     'L0_ffn_ln_b': (0.0, 0.1),
     'L0_ffn_gate_b': (0.0, 0.1),
     'L0_ffn_b1': (0.0, 0.1),
     'L0_ffn_b2': (0.0, 0.1)}
    factors = {}
    for name, (base, spread) in spreads.items():
        noise = np.random.default_rng([zlib.crc32(name.encode()), seed]).standard_normal(out[name].shape)
        drawn = base * np.exp(spread * noise) if base else spread * noise
        out[name] = jnp.asarray(drawn.astype(out[name].dtype))
    for name, factor in factors.items():
        out[name] = (out[name] * factor).astype(out[name].dtype)
    return out
```

```python
from contextlib import ExitStack

import numpy as np

import concourse.bass as bass
from concourse import mybir

F32 = mybir.dt.float32
BF16 = mybir.dt.bfloat16
ALU = mybir.AluOpType
ACT = mybir.ActivationFunctionType
AX = mybir.AxisListType

P = 128
B, T, D = 4, 512, 128
NT = T // P
NH, HD = 16, 8
NPAIR = NH // 2
NG = NH // 4
LAT = 64
NE, HID = 4, 512
NC = HID // P
NCH = NE * NC
SLOT_Q = (0, 0, 0, 1, 1, 2)
SLOT_K = (0, 1, 2, 0, 1, 0)
MAXROW = 8 * len(SLOT_Q)
PCOLS = 1280
KT_AT = {0: (0, 0), 1: (512, 128), 3: (896, 384), 2: (1024, 256)}
MASKED = -1e30
SCALE = float(1.0 / np.sqrt(HD))
LN_EPS, RMS_EPS, COS_EPS = 1e-5, 1e-6, 1e-8
RECIP_CAP = 1e18


class Signal:

    def __init__(self, sem, ffn, mid=0):
        self.sem, self.ffn, self.mid = sem, ffn, mid

    def at(self, part, n):
        kind, layer, b = part
        if layer == 0:
            return b * self.ffn + n + 1
        base = B * self.ffn + n + 1 + (self.mid if kind == "ffn" else 0)
        return b * (self.ffn + self.mid) + base


DVE_FFN, DVE_MID = 18, 9


def program(nc, x_in, out, w):
    ctx = ExitStack()
    with ctx:
        def sb(name, shape, dt=F32):
            return ctx.enter_context(nc.sbuf_tensor(name, shape, dt))

        def sem(name):
            return ctx.enter_context(nc.semaphore(name))

        signals = []

        def signal(name, ffn, mid=0):
            signals.append(Signal(sem(name), ffn, mid))
            return signals[-1]

        between = nc.dram_tensor("between", [B, T, D], F32, kind="Internal").ap()
        q_parts_d = nc.dram_tensor("q_parts_d", [3, P, T], BF16, kind="Internal").ap()
        k_parts_d = nc.dram_tensor("k_parts_d", [3, P, T], BF16, kind="Internal").ap()
        nmax_d = nc.dram_tensor("nmax_d", [3 * NH, T], BF16, kind="Internal").ap()

        wq = sb("wq", [P, 2, P])
        wdkv = sb("wdkv", [P, LAT])
        wukv_raw = sb("wukv_raw", [LAT, 2 * P])
        lat_affine = sb("lat_affine", [LAT, P])
        wk = sb("wk", [P, 2, P])
        wv = sb("wv", [P, P])
        wo = sb("wo", [P, P])
        gate = sb("gate", [P, NE])
        gate_b = sb("gate_b", [P, NE])
        w1 = sb("w1", [P, NE * HID])
        w2 = sb("w2", [P, NCH, D])
        b1 = sb("b1", [P, NCH])
        b2 = sb("b2", [NE, D])
        relu_b1 = sb("relu_b1", [P, NCH])
        relu_b1_by_e = sb("relu_b1_by_e", [P, NCH, NE])
        idle_sum = sb("idle_sum", [P, 1])
        own_bias = sb("own_bias", [NE, D])
        n1w = sb("n1w", [P, 1])
        n2w = sb("n2w", [P, 1])
        lng = sb("lng", [LAT, 1])
        lnb = sb("lnb", [LAT, 1])
        cos = sb("cos", [P, T])
        sin = sb("sin", [P, T])
        ident = sb("ident", [P, P])
        ident_b = sb("ident_b", [P, P], BF16)
        mask_q = sb("mask_q", [P, P], BF16)
        mask_k = sb("mask_k", [P, P], BF16)
        sel_e = sb("sel_e", [NE, NE, P], BF16)
        rank = sb("rank", [P, NT, NE])
        half_pow = sb("half_pow", [P, 8])

        x = sb("x", [P, NT, D])
        u = sb("u", [P, NT, D + 1])
        n = sb("n", [P, NT, D])
        stats = sb("stats", [P, NT, 6])
        mv = sb("mv", [P, NT, 2])
        met = sb("met", [P, 1])
        zero = sb("zero", [P, 1])
        powin = sb("powin", [P, 8])
        powout = sb("powout", [P, 8])
        nT = sb("nT", [P, T])
        zn = sb("zn", [P, NT, P])
        znT = sb("znT", [P, T])
        rope_a = sb("rope_a", [P, 2, T])
        rope_b = sb("rope_b", [P, 2, T])
        qk = sb("qk", [P, 2, T])
        rest = sb("rest", [P, 2, T])
        parts = sb("parts", [P, 2, 3, T], BF16)
        qs = sb("qs", [P, NPAIR, T], BF16)
        kz = sb("kz", [P, NH, T], BF16)
        v = sb("v", [P, NT, NH, 32])
        nmax = sb("nmax", [P, NT, NH])
        nmax_rest = sb("nmax_rest", [P, NT, NH])
        nmax_parts = sb("nmax_parts", [P, NT, P], BF16)
        nmaxT = sb("nmaxT", [3 * NH, T], BF16)
        pT = sb("pT", [P, 2, 4, PCOLS])
        oT_raw = sb("oT_raw", [P, NG, T])
        recip = sb("recip", [P, NT, 4])
        o = sb("o", [P, NT, D])
        oT = sb("oT", [P, T])
        x2 = sb("x2", [P, NT, D])
        square = sb("square", [P, D])
        n2 = sb("n2", [P, NT, D])
        n2T = sb("n2T", [P, T])
        base = sb("base", [P, NT, D])
        logit = sb("logit", [P, NT, NE])
        top = sb("top", [P, NT])
        onehot = sb("onehot", [P, NT, NE])
        ohT = sb("ohT", [NE, T])
        ohT_b = sb("ohT_b", [NE, T], BF16)
        xe = sb("xe", [P, NE, T])
        hid = sb("hid", [P, 4, T])
        yT = sb("yT", [P, T])
        res = sb("res", [P, NT, D])
        rnorm = sb("rnorm", [P, NT])
        rnorm_w = sb("rnorm_w", [P, NT, P])
        rrow = sb("rrow", [P, T])
        sim = xe
        esim = hid

        SC = [ctx.enter_context(nc.psum_tensor(f"score{i}", [P, 2, 512], F32)) for i in range(2)]
        W = [ctx.enter_context(nc.psum_tensor(f"work{i}", [P, 512], F32)) for i in range(2)]
        A = [ctx.enter_context(nc.psum_tensor(f"accum{i}", [P, 512], F32)) for i in range(2)]

        loads = sem("loads")
        ones_loaded = sem("ones_loaded")
        setup_pe = sem("setup_pe")
        setup_dve = sem("setup_dve")
        setup_pool = sem("setup_pool")
        x_loaded = signal("x_loaded", 16, 0)
        pow_in = signal("pow_in", 3, 2)
        pow_out = signal("pow_out", 3, 2)
        dve_step = signal("dve_step", 0)
        pool_step = signal("pool_step", 6)
        n_ready = signal("n_ready", 1)
        u_ready = signal("u_ready", 1, 1)
        qk_ready = signal("qk_ready", 2)
        parts_ready = signal("parts_ready", 2)
        parts_stored = signal("parts_stored", 32)
        stacks_loaded = signal("stacks_loaded", 16 * 26)
        nmax_ready = signal("nmax_ready", 1)
        nmax_stored = signal("nmax_stored", 16)
        nmax_loaded = signal("nmax_loaded", 32)
        sc_full = [signal(f"sc_full{i}", 28) for i in range(2)]
        sc_free = [signal(f"sc_free{i}", 28) for i in range(2)]
        w_full = [signal(f"w_full{i}", 19, 3) for i in range(2)]
        w_free = [signal(f"w_free{i}", 19, 3) for i in range(2)]
        a_full = [signal(f"a_full{i}", 3 - i, 1) for i in range(2)]
        a_free = [signal(f"a_free{i}", 2, 1) for i in range(2)]
        n2_ready = signal("n2_ready", 1)
        onehot_ready = signal("onehot_ready", 1)
        y_step = signal("y_step", NCH)
        yT_ready = signal("yT_ready", 1)
        res_ready = signal("res_ready", 1)
        out_stored = signal("out_stored", 16)
        rnorm_ready = signal("rnorm_ready", 0, 1)
        mid_loaded = sem("mid_loaded")
        setup_steps = sem("setup_steps")
        exp_ready = signal("exp_ready", 0, 4)
        x_new = signal("x_new", 0, 1)
        dve_step.ffn, dve_step.mid = DVE_FFN, DVE_MID

        block = ctx.enter_context(nc.Block())

        (T_N, LATENT, Q, QR, T_Z, K, KR, V, T_NMAX) = range(9)
        T_OUT = 9
        T_O, WO, T_N2, LOGIT, T_OH = range(13, 18)
        MASK = 18
        HIDDEN = 22
        N_STEP = HIDDEN + NCH
        (T_U, RROW, DOTS) = range(3)

        def full(eng, part, k):
            eng.wait_ge(w_full[k % 2].sem, w_full[k % 2].at(part, k // 2 + 1))

        def free(eng, part, k):
            eng.wait_ge(w_free[k % 2].sem, w_free[k % 2].at(part, k // 2 + 1))

        @block.sync
        def _(sp):
            for s in signals:
                sp.sem_inc(s.sem, 1)
            for dst, src in ((wq[:, 0, :], w["WqT"]), (wdkv[:, :], w["WdkvT"]), (wukv_raw[:, 0:P], w["WukT"]),
                             (wukv_raw[:, P:], w["WuvT"]), (wo[:, :], w["WoT"]), (gate[:, :], w["gateT"]),
                             (gate_b[:, :], w["gate_b"].to_broadcast([P, NE])), (b1[:, :], w["b1T"]),
                             (b2[:, :], w["b2"]), (n1w[:, :], w["n1"]), (n2w[:, :], w["n2"]), (lng[:, :], w["ln_g"]),
                             (lnb[:, :], w["ln_b"]), (cos[:, :], w["cos"]), (sin[:, :], w["sin"]),
                             (w1[:, :], w["W1T"]), (w2[:, :, :], w["W2T"])):
                sp.dma_start(dst, src).then_inc(loads, 16)
            sp.wait_ge(setup_pool, 1)
            for j in range(2):
                rows = kz[:, :, :].rearrange("r (p j) n -> r j p n", j=2)[64 * j + MAXROW:64 * j + MAXROW + 3, j]
                sp.dma_start(rows, w["ones"]).then_inc(ones_loaded, 16)

            def ffn(part):
                _, layer, b = part
                if layer == 0:
                    sp.wait_ge(res_ready.sem, res_ready.at(part, 0))
                    sp.dma_start(x[:, :, :], x_in[b].rearrange("(t p) d -> p t d", p=P)).then_inc(x_loaded.sem, 16)
                for s, (dst, q) in enumerate(((q_parts_d, 0), (k_parts_d, 1))):
                    sp.wait_ge(parts_ready.sem, parts_ready.at(part, s + 1))
                    sp.dma_start(dst.rearrange("s p n -> p s n"), parts[:, q]).then_inc(parts_stored.sem, 16)
                for i in range(2):
                    sp.wait_ge(sc_full[i].sem, sc_full[i].at(part, 0))
                sp.wait_ge(parts_stored.sem, parts_stored.at(part, 32))
                for j in range(2):
                    r = 64 * j
                    qd = q_parts_d.rearrange("s (p j d) n -> s j d p n", j=2, d=HD)
                    kd = k_parts_d.rearrange("s (p j d) n -> s j d p n", j=2, d=HD)
                    kzj = kz[:, :, :].rearrange("r (p j) n -> r j p n", j=2)
                    for s in range(6):
                        sp.dma_start(qs[r + 8 * s:r + 8 * s + 8, :, :], qd[SLOT_Q[s], j]).then_inc(stacks_loaded.sem, 16)
                    sp.dma_start(qs[r + MAXROW:r + MAXROW + 3, :, :], w["zeros"]).then_inc(stacks_loaded.sem, 16)
                for j in range(2):
                    r = 64 * j
                    for s in range(6):
                        sp.dma_start(kzj[r + 8 * s:r + 8 * s + 8, j], kd[SLOT_K[s], j]).then_inc(stacks_loaded.sem, 16)
                free(sp, part, T_NMAX)
                sp.dma_start(nmax_d, nmaxT[:, :]).then_inc(nmax_stored.sem, 16)
                sp.wait_ge(nmax_stored.sem, nmax_stored.at(part, 16))
                for j in range(2):
                    r = 64 * j + MAXROW
                    sp.dma_start(qs[r:r + 3, :, :], nmax_d.rearrange("(s p j) n -> j s p n", s=3, j=2)[j])\
                      .then_inc(nmax_loaded.sem, 16)
                sp.wait_ge(res_ready.sem, res_ready.at(part, 1))
                dst = between if layer == 0 else out
                sp.dma_start(dst[b].rearrange("(t p) d -> p t d", p=P), res[:, :, :]).then_inc(out_stored.sem, 16)

            with sp.Fori(0, B) as b:
                ffn(("ffn", 0, b))
            sp.wait_ge(out_stored.sem, 16 * B + 1)
            with sp.Fori(0, B) as b:
                part = ("mid", 1, b)
                sp.wait_ge(res_ready.sem, res_ready.at(part, 0))
                sp.dma_start(x[:, :, :], between[b].rearrange("(t p) d -> p t d", p=P)).then_inc(mid_loaded, 16)
                ffn(("ffn", 1, b))
            sp.wait_ge(out_stored.sem, 2 * 16 * B + 1)

        @block.gpsimd
        def _(pool):
            pool.memset(half_pow[:, :], -0.5)
            pool.memset(zero[:, :], 0.0)
            pool.memset(nmax_parts[:, :, :], 0.0)
            pool.memset(ident[:, :], 0.0)
            pool.memset(ident_b[:, :], 0.0)
            pool.memset(mask_q[:, :], 0.0)
            pool.memset(mask_k[:, :], 0.0)
            pool.memset(sel_e[:, :, :], 0.0)
            pool.memset(lat_affine[:, :], 0.0)
            pool.memset(zn[:, :, :], 0.0)
            pool.memset(kz[:, :, :], 0.0)
            pool.memset(qs[:, :, :], 0.0)
            pool.memset(v[:, :, :, :], 0.0)
            for e in range(NE):
                pool.memset(rank[:, :, e:e + 1], float(NE - e))
            pool.memset(relu_b1_by_e[:, :, :], 0.0)
            pool.memset(u[:, :, D:D + 1], 1.0).then_inc(setup_pool, 1)
            pool.wait_ge(setup_pool, 1)
            pool.memset(zn[:, :, LAT:LAT + 1], 1.0)
            pool.memset(v[:, :, :, HD:HD + 1], 1.0)
            for m in (ident, ident_b):
                pool.affine_select(out=m[:, :], in_=m[:, :], compare_op=ALU.not_equal, fill=1.0, base=0,
                                   pattern=[[-1, P]], channel_multiplier=1)
            pool.affine_select(out=mask_q[:, :], in_=mask_q[:, :], compare_op=ALU.is_ge, fill=MASKED, base=0,
                               pattern=[[-1, P]], channel_multiplier=1)
            pool.affine_select(out=mask_k[:, :], in_=mask_k[:, :], compare_op=ALU.is_ge, fill=MASKED, base=0,
                               pattern=[[1, P]], channel_multiplier=-1)
            last = pool.affine_select(out=sel_e[:, :, :], in_=sel_e[:, :, :], compare_op=ALU.not_equal, fill=1.0, base=0,
                               pattern=[[-1, NE], [0, P]], channel_multiplier=1)
            last.then_inc(setup_pool, 1)

            def power(part, k, cols):
                pool.wait_ge(pow_in.sem, pow_in.at(part, k + 1))
                pool.tensor_tensor(powout[:, 0:cols], powin[:, 0:cols], half_pow[:, 0:cols], ALU.pow)\
                    .then_inc(pow_out.sem, 1)

            def split(part, s):
                zeros = zero[:, 0:1].to_broadcast([P, T])
                pool.wait_ge(parts_stored.sem, parts_stored.at(part, 0))
                pool.wait_ge(qk_ready.sem, qk_ready.at(part, s + 1))
                pool.tensor_tensor(parts[:, s, 0, :], qk[:, s, :], zeros, ALU.add).then_inc(pool_step.sem, 1)
                pool.wait_ge(pool_step.sem, pool_step.at(part, 3 * s + 1))
                pool.tensor_tensor(rest[:, s, :], qk[:, s, :], parts[:, s, 0, :], ALU.subtract).then_inc(pool_step.sem, 1)
                pool.wait_ge(pool_step.sem, pool_step.at(part, 3 * s + 2))
                pool.tensor_tensor(parts[:, s, 1, :], rest[:, s, :], zeros, ALU.add).then_inc(pool_step.sem, 1)
                pool.wait_ge(pool_step.sem, pool_step.at(part, 3 * s + 3))
                pool.tensor_tensor(parts[:, s, 2, :], rest[:, s, :], parts[:, s, 1, :], ALU.subtract)\
                    .then_inc(parts_ready.sem, 1)

            def ffn(part):
                power(part, 0, 8)
                power(part, 1, 4)
                split(part, 0)
                split(part, 1)
                power(part, 2, 4)

            with pool.Fori(0, B) as b:
                ffn(("ffn", 0, b))
            with pool.Fori(0, B) as b:
                mid = ("mid", 1, b)
                power(mid, 0, 4)
                power(mid, 1, 4)
                ffn(("ffn", 1, b))

        @block.scalar
        def _(act):
            def copy_work(part, k, dst, src):
                full(act, part, k)
                nc.scalar.activation(dst, src, ACT.Copy).then_inc(w_free[k % 2].sem, 1)

            def ffn(part):
                copy_work(part, T_N, nT[:, :], W[T_N % 2][:, :])
                copy_work(part, T_Z, znT[:, :], W[T_Z % 2][:, :])
                full(act, part, V)
                nc.scalar.activation(v[:, :, :, 0:HD],
                                     W[V % 2][:, :].rearrange("p (t h d) -> p t h d", t=NT, d=HD), ACT.Copy)\
                    .then_inc(w_free[V % 2].sem, 1)
                full(act, part, T_NMAX)
                nc.scalar.activation(nmaxT[:, :], W[T_NMAX % 2][0:3 * NH, :].bitcast(BF16)[:, 0:T], ACT.Copy)\
                    .then_inc(w_free[T_NMAX % 2].sem, 1)
                for p in range(NPAIR):
                    g, half = p // 2, 2 * (p % 2)
                    if p % 2 == 0:
                        act.wait_ge(a_full[g % 2].sem, a_full[g % 2].at(part, g // 2))
                    for z in range(3):
                        unit = 3 * p + z
                        sc = unit % 2
                        act.wait_ge(sc_full[sc].sem, sc_full[sc].at(part, 16 + unit // 2 + 1))
                        if z < 2:
                            ins = nc.scalar.activation(pT[:, g % 2, half + z, 0:1024],
                                                       SC[sc][:, :, :].rearrange("p a n -> p (a n)"), ACT.Exp, scale=SCALE)
                        else:
                            ins = nc.scalar.activation(pT[:, g % 2, half:half + 2, 1024:PCOLS],
                                                       SC[sc][:, 0, :].rearrange("p (j n) -> p j n", j=2),
                                                       ACT.Exp, scale=SCALE)
                        ins.then_inc(sc_free[sc].sem, 1)
                copy_work(part, T_O, oT[:, :], W[T_O % 2][:, :])
                copy_work(part, T_N2, n2T[:, :], W[T_N2 % 2][:, :])
                full(act, part, T_OH)
                nc.scalar.activation(ohT[:, :], W[T_OH % 2][0:NE, :], ACT.Copy)
                nc.scalar.activation(ohT_b[:, :], W[T_OH % 2][0:NE, :], ACT.Copy).then_inc(w_free[T_OH % 2].sem, 1)
                for c in range(0, NCH, 2):
                    full(act, part, HIDDEN + c)
                    if c >= 4:
                        act.wait_ge(y_step.sem, y_step.at(part, c - 3))
                    nc.scalar.activation(hid[:, c % 4, :], W[(HIDDEN + c) % 2][:, :], ACT.Relu, bias=b1[:, c:c + 1])\
                        .then_inc(w_free[(HIDDEN + c) % 2].sem, 1)

            act.wait_ge(loads, 16 * 17)
            with act.Fori(0, B) as b:
                ffn(("ffn", 0, b))
            with act.Fori(0, B) as b:
                mid = ("mid", 1, b)
                copy_work(mid, T_U, nT[:, :], W[T_U % 2][:, :])
                copy_work(mid, RROW, rrow[:, :], W[RROW % 2][:, :])
                for t in range(NT):
                    free(act, mid, DOTS + t)
                    nc.scalar.activation(esim[:, t, :], sim[:, t, :], ACT.Exp).then_inc(exp_ready.sem, 1)
                ffn(("ffn", 1, b))

        @block.tensor
        def _(pe):
            pe.wait_ge(setup_dve, 1)
            pe.matmul(W[0][:, 0:2 * P], lat_affine[:, :], wukv_raw[:, :], start=True, stop=True).then_inc(setup_pe, 1)
            for c in range(NCH):
                pe.matmul(W[1][:, 0:1], w2[:, c, :], relu_b1[:, c:c + 1], start=(c == 0), stop=(c == NCH - 1))
            for c in range(NCH):
                last = pe.matmul(A[0][0:NE, 0:D], relu_b1_by_e[:, c, :], w2[:, c, :],
                                 start=(c == 0), stop=(c == NCH - 1))
            last.then_inc(setup_pe, 1)
            pe.wait_ge(setup_dve, 2)

            def step(part, k, emit):
                f = w_free[k % 2]
                pe.wait_ge(f.sem, f.at(part, k // 2))
                emit(W[k % 2]).then_inc(w_full[k % 2].sem, 1)

            def transposes(src):
                def emit(bank):
                    for t in range(NT):
                        last = pe.transpose(bank[:, t * P:(t + 1) * P], src(t), ident[:, :])
                    return last
                return emit

            def product(lhsT, rhs, cols):
                return lambda bank: pe.matmul(bank[:, 0:cols], lhsT, rhs, start=True, stop=True)

            def by_token(src, weight, cols):
                def emit(bank):
                    for t in range(NT):
                        last = pe.matmul(bank[:, t * cols:(t + 1) * cols], src[:, t * P:(t + 1) * P], weight,
                                         start=True, stop=True)
                    return last
                return emit

            def max_unit(part, unit):
                p, qt = unit // NT, unit % NT
                sc, cols = unit % 2, (qt + 1) * P
                pe.wait_ge(sc_free[sc].sem, sc_free[sc].at(part, unit // 2))
                for j in range(2):
                    pe.matmul(SC[sc][:, j, 0:cols], qs[:, p, qt * P:(qt + 1) * P], kz[:, 2 * p + j, 0:cols],
                              start=True, stop=False)
                    last = pe.matmul(SC[sc][:, j, cols - P:cols], ident_b[:, :], mask_q[:, :], start=False, stop=True)
                last.then_inc(sc_full[sc].sem, 1)

            def key_tile(bank, at, p, h, kt):
                q0 = kt * P
                pe.matmul(bank[:, at:at + T - q0], kz[:, h, q0:q0 + P], qs[:, p, q0:T], start=True, stop=False)
                return pe.matmul(bank[:, at:at + P], ident_b[:, :], mask_k[:, :], start=False, stop=True)

            def score_unit(part, unit):
                p, z = unit // 3, unit % 3
                sc = unit % 2
                pe.wait_ge(sc_free[sc].sem, sc_free[sc].at(part, 16 + unit // 2))
                if z < 2:
                    h = 2 * p + z
                    key_tile(SC[sc][:, 0], 0, p, h, 0)
                    key_tile(SC[sc][:, 1], 0, p, h, 1)
                    last = key_tile(SC[sc][:, 1], 384, p, h, 3)
                else:
                    key_tile(SC[sc][:, 0], 0, p, 2 * p, 2)
                    last = key_tile(SC[sc][:, 0], 256, p, 2 * p + 1, 2)
                last.then_inc(sc_full[sc].sem, 1)

            def weighted_sum(part, g):
                a = g % 2
                for sc in range(2):
                    units = [q for q in range(6 * g, 6 * g + 6) if q % 2 == sc]
                    pe.wait_ge(sc_free[sc].sem, sc_free[sc].at(part, 16 + units[-1] // 2 + 1))
                pe.wait_ge(a_free[a].sem, a_free[a].at(part, g // 2))
                if g < 2:
                    last_read = (res_ready, yT_ready)[g]
                    pe.wait_ge(last_read.sem, last_read.at(part, 0))
                for i, (kt, (at, q0)) in enumerate(KT_AT.items()):
                    for j in range(4):
                        last = pe.matmul(A[a][32 * j:32 * j + 32, q0:T], v[:, kt, 4 * g + j, :],
                                         pT[:, a, j, at:at + T - q0], start=(i == 0), stop=(i == NT - 1))
                last.then_inc(a_full[a].sem, 1)

            def turn_out(part, g):
                pe.wait_ge(a_free[g % 2].sem, a_free[g % 2].at(part, g // 2 + 1))
                step(part, T_OUT + g, transposes(lambda t: oT_raw[:, g, t * P:(t + 1) * P]))

            def ffn(part):
                pe.wait_ge(n_ready.sem, n_ready.at(part, 1))
                step(part, T_N, transposes(lambda t: n[:, t, :]))
                free(pe, part, T_N)
                step(part, LATENT, by_token(nT, wdkv[:, :], LAT))
                step(part, Q, product(wq[:, 0, :], nT[:, :], T))
                free(pe, part, LATENT)
                step(part, QR, product(wq[:, 1, :], nT[:, :], T))
                step(part, T_Z, transposes(lambda t: zn[:, t, :]))
                free(pe, part, T_Z)
                step(part, K, product(wk[:, 0, :], znT[:, :], T))
                step(part, KR, product(wk[:, 1, :], znT[:, :], T))
                step(part, V, by_token(znT, wv[:, :], P))
                pe.wait_ge(stacks_loaded.sem, stacks_loaded.at(part, stacks_loaded.ffn))
                for unit in range(NPAIR * NT):
                    max_unit(part, unit)
                pe.wait_ge(nmax_ready.sem, nmax_ready.at(part, 1))

                def turn_max(bank):
                    for t in range(NT):
                        last = pe.transpose(bank[:, :].bitcast(BF16)[:, t * P:(t + 1) * P], nmax_parts[:, t, :],
                                            ident_b[:, :])
                    return last
                step(part, T_NMAX, turn_max)
                free(pe, part, V)
                pe.wait_ge(nmax_loaded.sem, nmax_loaded.at(part, 32))
                for unit in range(3 * NPAIR):
                    score_unit(part, unit)
                    if unit >= 7 and (unit - 7) % 6 == 0:
                        weighted_sum(part, (unit - 7) // 6)
                    if unit >= 10 and (unit - 10) % 6 == 0:
                        turn_out(part, (unit - 10) // 6)
                weighted_sum(part, NG - 1)
                turn_out(part, NG - 1)
                for g in (NG - 2, NG - 1):
                    free(pe, part, T_OUT + g)
                step(part, T_O, transposes(lambda t: o[:, t, :]))
                free(pe, part, T_O)
                step(part, WO, by_token(oT, wo[:, :], D))
                pe.wait_ge(n2_ready.sem, n2_ready.at(part, 1))
                step(part, T_N2, transposes(lambda t: n2[:, t, :]))
                free(pe, part, T_N2)
                step(part, LOGIT, by_token(n2T, gate[:, :], NE))
                pe.wait_ge(onehot_ready.sem, onehot_ready.at(part, 1))

                def turn_onehot(bank):
                    for t in range(NT):
                        last = pe.transpose(bank[0:NE, t * P:(t + 1) * P], onehot[:, t, :], ident[:, :])
                    return last
                step(part, T_OH, turn_onehot)
                free(pe, part, T_OH)
                for e in range(NE):
                    step(part, MASK + e, product(sel_e[:, e, :], ohT_b[:, :], T))
                pe.wait_ge(a_free[1].sem, a_free[1].at(part, 2))
                pe.matmul(A[1][:, :], own_bias[:, :], ohT[:, :], start=True, stop=False)

                def second(c):
                    free(pe, part, HIDDEN + c)
                    last = pe.matmul(A[1][:, :], w2[:, c, :], hid[:, c % 4, :], start=False, stop=(c == NCH - 1))
                    last.then_inc(y_step.sem, 1)
                for c in range(NCH):
                    if c % NC == 0:
                        free(pe, part, MASK + c // NC)
                    step(part, HIDDEN + c, product(w1[:, c * P:(c + 1) * P], xe[:, c // NC, :], T))
                    if c:
                        second(c - 1)
                second(NCH - 1)
                pe.wait_ge(yT_ready.sem, yT_ready.at(part, 1))
                for t in range(NT):
                    last = pe.transpose(A[0][:, t * P:(t + 1) * P], yT[:, t * P:(t + 1) * P], ident[:, :])
                last.then_inc(a_full[0].sem, 1)

            def mid(part):
                pe.wait_ge(u_ready.sem, u_ready.at(part, 1))
                step(part, T_U, transposes(lambda t: u[:, t, 0:D]))
                pe.wait_ge(rnorm_ready.sem, rnorm_ready.at(part, 1))

                def norm_rows(bank):
                    for t in range(NT):
                        last = pe.matmul(bank[:, t * P:(t + 1) * P], rnorm_w[:, t, :], ident[:, :], start=True, stop=True)
                    return last
                step(part, RROW, norm_rows)
                free(pe, part, T_U)
                for t in range(NT):
                    step(part, DOTS + t, product(nT[:, t * P:(t + 1) * P], nT[:, :], T))
                pe.wait_ge(exp_ready.sem, exp_ready.at(part, NT))
                for a in range(2):
                    last_read = (res_ready, yT_ready)[a]
                    pe.wait_ge(last_read.sem, last_read.at(part, 0))
                    for i in range(2):
                        q0 = (2 * a + i) * P
                        for t in range(NT):
                            last = pe.matmul(A[a][:, i * (D + 1):(i + 1) * (D + 1)], esim[:, t, q0:q0 + P], u[:, t, :],
                                             start=(t == 0), stop=(t == NT - 1))
                    last.then_inc(a_full[a].sem, 1)

            with pe.Fori(0, B) as b:
                ffn(("ffn", 0, b))
            with pe.Fori(0, B) as b:
                mid(("mid", 1, b))
                ffn(("ffn", 1, b))

        @block.vector
        def _(dve):
            V_ = nc.vector

            class Chain:
                part, n = None, 0

            def begin(part):
                Chain.part, Chain.n = part, 0

            def then(ins):
                ins.then_inc(dve_step.sem, 1)
                Chain.n += 1
                dve.wait_ge(dve_step.sem, dve_step.at(Chain.part, Chain.n))

            dve.wait_ge(loads, 16 * 17)
            dve.wait_ge(setup_pool, 2)
            dve.wait_ge(ones_loaded, 32)
            steps = [0]

            def link(ins):
                ins.then_inc(setup_steps, 1)
                steps[0] += 1
                dve.wait_ge(setup_steps, steps[0])
            V_.tensor_scalar(lat_affine[:, 0:LAT], ident[0:LAT, 0:LAT], lng[:, 0:1], None, ALU.mult)
            V_.tensor_copy(lat_affine[:, LAT:LAT + 1], lnb[:, :])
            V_.tensor_scalar(wq[:, 0, :], wq[:, 0, :], n1w[:, 0:1], None, ALU.mult)
            V_.tensor_scalar(wdkv[:, :], wdkv[:, :], n1w[:, 0:1], None, ALU.mult)
            V_.tensor_scalar(gate[:, :], gate[:, :], n2w[:, 0:1], None, ALU.mult)
            V_.tensor_scalar(w1[:, :], w1[:, :], n2w[:, 0:1], None, ALU.mult)
            link(V_.tensor_scalar(relu_b1[:, :], b1[:, :], 0.0, None, ALU.max))
            for e in range(NE):
                last = V_.tensor_copy(relu_b1_by_e[:, e * NC:(e + 1) * NC, e:e + 1],
                                      relu_b1[:, e * NC:(e + 1) * NC].rearrange("p (c o) -> p c o", o=1))
            last.then_inc(setup_dve, 1)
            dve.wait_ge(setup_pe, 1)
            V_.tensor_copy(wk[:, 0, :], W[0][:, 0:P])
            link(V_.tensor_copy(wv[:, :], W[0][:, P:2 * P]))
            for m in (wq, wk):
                src = m[:, 0, :].rearrange("p (h d) -> p h d", d=HD)
                dst = m[:, 1, :].rearrange("p (h d) -> p h d", d=HD)
                V_.tensor_scalar(dst[:, :, 0:HD // 2], src[:, :, HD // 2:HD], -1.0, None, ALU.mult)
                V_.tensor_copy(dst[:, :, HD // 2:HD], src[:, :, 0:HD // 2])
            dve.wait_ge(setup_pe, 2)
            V_.tensor_copy(idle_sum[:, :], W[1][:, 0:1])
            V_.tensor_tensor(own_bias[:, :], A[0][0:NE, 0:D], b2[:, :], ALU.add).then_inc(setup_dve, 1)
            dve.wait_ge(setup_dve, 2)

            def moments(src, cols):
                for t in range(NT):
                    ins = V_.bn_stats(stats[:, t, :], src(t))
                then(ins)
                V_.tensor_copy(met[:, :], stats[:, 0, 0:1])
                for t in range(NT):
                    ins = V_.bn_aggr(mv[:, t, :], stats[:, t, :])
                then(ins)

            def layer_norm(part, k):
                moments(lambda t: x[:, t, :], D)
                if part[0] == "ffn":
                    V_.tensor_scalar(powin[:, 4:8], mv[:, :, 1], 1.0 + RMS_EPS, RMS_EPS * LN_EPS, ALU.mult, ALU.add)
                V_.tensor_scalar(powin[:, 0:4], mv[:, :, 1], LN_EPS, None, ALU.add).then_inc(pow_in.sem, 1)
                dve.wait_ge(pow_out.sem, pow_out.at(part, k + 1))
                if part[0] == "ffn":
                    for t in range(NT):
                        ins = V_.tensor_scalar(n[:, t, :], x[:, t, :], mv[:, t, 0:1], powout[:, 4 + t:5 + t],
                                               ALU.subtract, ALU.mult)
                    ins.then_inc(n_ready.sem, 1)
                for t in range(NT):
                    ins = V_.tensor_scalar(u[:, t, 0:D], x[:, t, :], mv[:, t, 0:1], powout[:, t:t + 1],
                                           ALU.subtract, ALU.mult)
                ins.then_inc(u_ready.sem, 1)
                dve.wait_ge(u_ready.sem, u_ready.at(part, 1))

            def rope(part, s, k):
                full(dve, part, k)
                V_.tensor_tensor(rope_a[:, s, :], W[k % 2][:, :], cos[:, :], ALU.mult).then_inc(w_free[k % 2].sem, 1)
                full(dve, part, k + 1)
                V_.tensor_tensor(rope_b[:, s, :], W[(k + 1) % 2][:, :], sin[:, :], ALU.mult)\
                    .then_inc(w_free[(k + 1) % 2].sem, 1)
                free(dve, part, k)
                free(dve, part, k + 1)
                V_.tensor_tensor(qk[:, s, :], rope_a[:, s, :], rope_b[:, s, :], ALU.add).then_inc(qk_ready.sem, 1)

            def ffn(part):
                if part[1] == 0:
                    begin(part)
                    dve.wait_ge(x_loaded.sem, x_loaded.at(part, 16))
                else:
                    begin(part)
                    dve.wait_ge(x_new.sem, x_new.at(part, 0))
                layer_norm(part, 0)
                full(dve, part, LATENT)
                lat = W[LATENT % 2][:, 0:NT * LAT].rearrange("p (t c) -> p t c", t=NT)
                moments(lambda t: lat[:, t, :], LAT)
                V_.tensor_scalar(powin[:, 0:4], mv[:, :, 1], LN_EPS, None, ALU.add).then_inc(pow_in.sem, 1)
                dve.wait_ge(pow_out.sem, pow_out.at(part, 2))
                for t in range(NT):
                    ins = V_.tensor_scalar(zn[:, t, 0:LAT], lat[:, t, :], mv[:, t, 0:1], powout[:, t:t + 1],
                                           ALU.subtract, ALU.mult)
                ins.then_inc(w_free[LATENT % 2].sem, 1)
                rope(part, 0, Q)
                rope(part, 1, K)
                for unit in range(NPAIR * NT):
                    p, qt = unit // NT, unit % NT
                    sc = unit % 2
                    dve.wait_ge(sc_full[sc].sem, sc_full[sc].at(part, unit // 2 + 1))
                    V_.tensor_reduce(nmax[:, qt, 2 * p:2 * p + 2], SC[sc][:, :, 0:(qt + 1) * P], AX.X, ALU.max,
                                     negate=True).then_inc(sc_free[sc].sem, 1)
                for sc in range(2):
                    dve.wait_ge(sc_free[sc].sem, sc_free[sc].at(part, 16))
                then(V_.tensor_copy(nmax_parts[:, :, 0:NH], nmax[:, :, :]))
                then(V_.tensor_tensor(nmax_rest[:, :, :], nmax[:, :, :], nmax_parts[:, :, 0:NH], ALU.subtract))
                then(V_.tensor_copy(nmax_parts[:, :, NH:2 * NH], nmax_rest[:, :, :]))
                V_.tensor_tensor(nmax_parts[:, :, 2 * NH:3 * NH], nmax_rest[:, :, :], nmax_parts[:, :, NH:2 * NH], ALU.subtract)\
                    .then_inc(nmax_ready.sem, 1)
                def out_copy(g):
                    dve.wait_ge(a_full[g % 2].sem, a_full[g % 2].at(part, g // 2 + 1))
                    V_.tensor_copy(oT_raw[:, g, :], A[g % 2][:, :]).then_inc(a_free[g % 2].sem, 1)

                def divide(g):
                    k = T_OUT + g
                    full(dve, part, k)
                    bank = W[k % 2][:, :].rearrange("p (t j c) -> p t j c", t=NT, c=32)
                    then(V_.reciprocal(recip[:, :, :], bank[:, :, :, HD]))
                    ins = V_.tensor_tensor(o[:, :, 4 * HD * g:4 * HD * (g + 1)].rearrange("p t (j d) -> p t j d", d=HD),
                                           bank[:, :, :, 0:HD],
                                           recip[:, :, :].unsqueeze(3).to_broadcast([P, NT, 4, HD]), ALU.mult)
                    ins.then_inc(w_free[k % 2].sem, 1)
                for g in range(NG):
                    out_copy(g)
                    divide(g)
                full(dve, part, WO)
                V_.tensor_tensor(x2[:, :, :], W[WO % 2][:, :].rearrange("p (t d) -> p t d", t=NT), u[:, :, 0:D], ALU.add)\
                    .then_inc(w_free[WO % 2].sem, 1)
                free(dve, part, WO)
                for t in range(NT):
                    ins = V_.tensor_tensor_reduce(square[:, :], x2[:, t, :], x2[:, t, :], 1.0 / D, RMS_EPS,
                                                  ALU.mult, ALU.add, powin[:, t:t + 1])
                    if t == NT - 1:
                        ins.then_inc(pow_in.sem, 1)
                    else:
                        then(ins)
                V_.scalar_tensor_tensor(out=base[:, :, :], in0=x2[:, :, :], scalar=0.5, in1=x[:, :, :],
                                        op0=ALU.mult, op1=ALU.add)
                dve.wait_ge(pow_out.sem, pow_out.at(part, 3))
                for t in range(NT):
                    ins = V_.tensor_scalar(n2[:, t, :], x2[:, t, :], powout[:, t:t + 1], None, ALU.mult)
                ins.then_inc(n2_ready.sem, 1)
                full(dve, part, LOGIT)
                V_.tensor_tensor(logit[:, :, :], W[LOGIT % 2][:, 0:NT * NE].rearrange("p (t e) -> p t e", t=NT),
                                 gate_b[:, :].unsqueeze(1).to_broadcast([P, NT, NE]), ALU.add)\
                    .then_inc(w_free[LOGIT % 2].sem, 1)
                free(dve, part, LOGIT)
                for last in (False, True):
                    then(V_.tensor_reduce(top[:, :], logit[:, :, :], AX.X, ALU.max))
                    ins = V_.tensor_tensor(onehot[:, :, :], logit[:, :, :],
                                           top[:, :].unsqueeze(2).to_broadcast([P, NT, NE]), ALU.is_equal)
                    if last:
                        ins.then_inc(onehot_ready.sem, 1)
                    else:
                        then(ins)
                        then(V_.tensor_tensor(logit[:, :, :], onehot[:, :, :], rank[:, :, :], ALU.mult))
                free(dve, part, T_N2)
                for e in range(NE):
                    full(dve, part, MASK + e)
                    V_.tensor_tensor(xe[:, e, :], n2T[:, :], W[(MASK + e) % 2][:, :], ALU.mult)\
                        .then_inc(w_free[(MASK + e) % 2].sem, 1)
                for c in range(1, NCH, 2):
                    full(dve, part, HIDDEN + c)
                    if c >= 4:
                        dve.wait_ge(y_step.sem, y_step.at(part, c - 3))
                    V_.tensor_scalar(hid[:, c % 4, :], W[(HIDDEN + c) % 2][:, :], b1[:, c:c + 1], 0.0, ALU.add, ALU.max)\
                        .then_inc(w_free[(HIDDEN + c) % 2].sem, 1)
                dve.wait_ge(y_step.sem, y_step.at(part, NCH))
                V_.tensor_scalar(yT[:, :], A[1][:, :], idle_sum[:, 0:1], None, ALU.subtract).then_inc(yT_ready.sem, 1)
                dve.wait_ge(a_full[0].sem, a_full[0].at(part, 3))
                dve.wait_ge(out_stored.sem, out_stored.at(part, 0))
                V_.scalar_tensor_tensor(out=res[:, :, :], in0=A[0][:, :].rearrange("p (t d) -> p t d", t=NT), scalar=0.5,
                                        in1=base[:, :, :], op0=ALU.mult, op1=ALU.add).then_inc(res_ready.sem, 1)
                assert Chain.n == DVE_FFN, Chain.n

            def mid(part):
                b = part[2]
                begin(part)
                dve.wait_ge(mid_loaded, b * 16 + 16)
                layer_norm(part, 0)
                for t in range(NT):
                    ins = V_.tensor_tensor_reduce(square[:, :], u[:, t, 0:D], u[:, t, 0:D], 1.0, 0.0,
                                                  ALU.mult, ALU.add, powin[:, t:t + 1])
                    if t == NT - 1:
                        ins.then_inc(pow_in.sem, 1)
                    else:
                        then(ins)
                dve.wait_ge(pow_out.sem, pow_out.at(part, 2))
                then(V_.tensor_scalar(rnorm[:, :], powout[:, 0:4], RECIP_CAP, None, ALU.min))
                V_.tensor_copy(rnorm_w[:, :, :], rnorm[:, :].unsqueeze(2).to_broadcast([P, NT, P]))\
                    .then_inc(rnorm_ready.sem, 1)
                free(dve, part, RROW)
                for t in range(NT):
                    ins = V_.tensor_scalar(sim[:, t, :], rrow[:, :], rnorm[:, t:t + 1], 1.0 / COS_EPS, ALU.mult, ALU.min)
                then(ins)
                for t in range(NT):
                    full(dve, part, DOTS + t)
                    V_.tensor_tensor(sim[:, t, :], sim[:, t, :], W[(DOTS + t) % 2][:, :], ALU.mult)\
                        .then_inc(w_free[(DOTS + t) % 2].sem, 1)
                for a in range(2):
                    dve.wait_ge(a_full[a].sem, a_full[a].at(part, 1))
                    bank = A[a][:, 0:2 * (D + 1)].rearrange("p (i c) -> p i c", i=2)
                    then(V_.reciprocal(recip[:, 0, 2 * a:2 * a + 2], bank[:, :, D]))
                    for i in range(2):
                        t = 2 * a + i
                        ins = V_.scalar_tensor_tensor(out=n[:, t, :], in0=bank[:, i, 0:D], scalar=recip[:, 0, t:t + 1],
                                                      in1=u[:, t, 0:D], op0=ALU.mult, op1=ALU.add)
                    ins.then_inc(a_free[a].sem, 1)
                for a in range(2):
                    dve.wait_ge(a_free[a].sem, a_free[a].at(part, 1))
                V_.tensor_tensor(x[:, :, :], x[:, :, :], n[:, :, :], ALU.add).then_inc(x_new.sem, 1)
                assert Chain.n == DVE_MID, Chain.n

            with dve.Fori(0, B) as b:
                ffn(("ffn", 0, b))
            with dve.Fori(0, B) as b:
                mid(("mid", 1, b))
                ffn(("ffn", 1, b))



def rope_tables():
    half = HD // 2
    inv_freq = (np.float32(1.0) / np.power(np.float32(10000.0), np.arange(half, dtype=np.float32) / np.float32(half)))
    angle = np.arange(T, dtype=np.float32)[None, :] * inv_freq.astype(np.float32)[:, None]
    rows = np.tile(angle.astype(np.float64), (P // half, 1))
    return np.cos(rows).astype(np.float32), np.sin(rows).astype(np.float32)


def kernel(**inputs):
    import numpy as _np
    import concourse.bacc as _bacc
    from concourse import mybir as _mybir
    from concourse.bass_utils import run_bass_kernel_spmd as _run

    g = {k: _np.asarray(a) for k, a in inputs.items()}
    f = lambda name: g["L0_ffn_" + name]
    cos, sin = rope_tables()
    arrays = {
        "x": g["L0_attn_x"],
        "WqT": f("Wq").T, "WdkvT": f("Wdkv").T, "WukT": f("Wuk").T, "WuvT": f("Wuv").T, "WoT": f("Wo").T,
        "gateT": f("gate_w").T, "gate_b": f("gate_b").reshape(1, NE),
        "b1T": f("b1").reshape(NCH, P).T, "b2": f("b2"),
        "n1": f("norm1_w").reshape(P, 1), "n2": f("norm2_w").reshape(P, 1),
        "ln_g": f("ln_g").reshape(LAT, 1), "ln_b": f("ln_b").reshape(LAT, 1),
        "W1T": f("W1").reshape(NE * HID, D).T,
        "W2T": f("W2").transpose(0, 2, 1).reshape(NCH, P, D).transpose(1, 0, 2),
        "ones": _np.ones((3, NPAIR, T), _mybir.dt.np(BF16)), "zeros": _np.zeros((3, NPAIR, T), _mybir.dt.np(BF16)),
        "cos": cos, "sin": sin,
    }
    nc = _bacc.Bacc("TRN2", target_bir_lowering=False, num_devices=1)
    arrays = {f"in_{k}": _np.ascontiguousarray(a) for k, a in arrays.items()}
    args = {k[3:]: nc.dram_tensor(k, a.shape, _mybir.dt.from_np(a.dtype), kind="ExternalInput").ap()
            for k, a in arrays.items()}
    out = nc.dram_tensor("out_0", (B, T, D), F32, kind="ExternalOutput").ap()
    program(nc, args.pop("x"), out, args)
    r = _run(nc, [arrays], core_ids=[0])
    return r.results[0]["out_0"]
```

```python
from contextlib import ExitStack

import numpy as np

import concourse.bass as bass
from concourse import mybir

F32 = mybir.dt.float32
BF16 = mybir.dt.bfloat16
ALU = mybir.AluOpType
ACT = mybir.ActivationFunctionType
AX = mybir.AxisListType

P = 128
B, T, D = 4, 512, 128
NT = T // P
NH, HD = 16, 8
NPAIR = NH // 2
NG = NH // 4
LAT = 64
NE, HID = 4, 512
NC = HID // P
NCH = NE * NC
NHALF = NPAIR // 2
SLOTS = ((0, 3, 0), (3, 2, 1), (5, 1, 2))
N_SLOT = sum(n for _, n, _ in SLOTS)
MAXROW = HD * N_SLOT
PCOLS = 1280
KT_AT = {0: (0, 0), 1: (512, 128), 3: (896, 384), 2: (1024, 256)}
MASKED = -1e30
SCALE = float(1.0 / np.sqrt(HD))
LN_EPS, RMS_EPS, COS_EPS = 1e-5, 1e-6, 1e-8
RECIP_CAP = 1e18


class Body:

    def __init__(self, kind, b=0):
        self.kind, self.b = kind, b

    def item(self, part):
        return {"front": {"START": 0, "BODY": self.b + 1, "BODY_MID": self.b + B},
                "back": {"BODY": self.b, "BODY_MID": self.b + B - 1, "END": 2 * B - 1},
                "mid": {"BODY_MID": self.b}}[part][self.kind]


class Signal:

    def __init__(self, sem, per):
        self.sem, self.per = sem, per

    def at(self, body, n):
        if isinstance(self.per, dict):
            per = self.per
            before = {"START": 0, "BODY": per["START"], "BODY_MID": per["START"] + (B - 1) * per["BODY"],
                      "END": per["START"] + (B - 1) * per["BODY"] + B * per["BODY_MID"]}[body.kind]
            each = 0 if body.kind in ("START", "END") else per[body.kind]
            return self.sem, body.b * each + (before + n + 1)
        part, each = self.per
        return self.sem, body.item(part) * each + (n + 1)

    def at_end_of(self, item):
        return self.sem, item * self.per[1] + (self.per[1] + 1)


BESIDE_SCORES = {
    "BODY": {4: ["T_N"], 6: ["LATENT"], 7: ["Q", ("sum", 0)], 8: ["QR"], 9: ["T_Z"], 10: ["T_OUT0"], 11: ["K"],
             12: ["KR"], 13: [("sum", 1)], 16: ["T_OUT1"], 19: [("sum", 2)], 22: ["T_OUT2"]},
    "BODY_MID": {3: ["T_U"], 4: ["RROW"], 5: ["DOTS0"], 6: ["DOTS1"], 7: ["DOTS2", ("sum", 0)], 8: ["DOTS3"],
                 9: ["AV0", "AV1", ("front", 0)], 10: ["T_OUT0"], 13: ["T_N", ("sum", 1)], 14: ["LATENT"], 15: ["Q"],
                 16: ["QR"], 17: ["T_Z", "T_OUT1"], 18: ["K"], 19: ["KR"], 20: [("sum", 2)], 23: ["T_OUT2"]},
    "END": {7: [("sum", 0)], 10: ["T_OUT0"], 13: [("sum", 1)], 16: ["T_OUT1"], 19: [("sum", 2)], 22: ["T_OUT2"]},
}
BESIDE_STEPS = {"T_O": 2, "WO": 3, "T_N2": 2, "LOGIT": 3, "T_OH": 2}
BESIDE_CHUNKS = 2
N_SCORE, N_MAX = 3 * NPAIR, NPAIR * NT


def events(kind):
    out = []

    def add(*names):
        out.extend(("work", x) if isinstance(x, str) else x for x in names)

    if kind == "START":
        add(("front", 0), "T_N", "LATENT", "Q", "QR", "T_Z", "K", "KR", "V")
        add(*(("max", m) for m in range(N_MAX)), ("nmax", 0), "T_NMAX")
        return out
    add(("save", 0))
    if kind == "BODY_MID":
        add(("mid", 0))
    elif kind == "BODY":
        add(("front", 0))
    for unit in range(N_SCORE):
        add(("score", unit))
        for x in BESIDE_SCORES[kind].get(unit, ()):
            add(x)
    add(("sum", NG - 1))
    nxt = kind != "END"
    if nxt:
        add("V")
    add("T_OUT3")
    m = 0

    def maxima(k):
        nonlocal m
        for _ in range(k if nxt else 0):
            if m < N_MAX:
                add(("max", m))
                m += 1
                if m == N_MAX:
                    add(("nmax", 0))
    for x in ("T_O", "WO", "T_N2", "LOGIT", "T_OH"):
        if x == "T_N2":
            add(("norm2", 0))
        add(x)
        maxima(BESIDE_STEPS[x])
    add(*(f"MASK{e}" for e in range(NE)))
    turned = not nxt
    for c in range(NCH):
        add(f"HIDDEN{c}")
        if c:
            add(("second", c - 1))
        if m == N_MAX and not turned:
            add("T_NMAX")
            turned = True
        maxima(BESIDE_CHUNKS)
    assert m == N_MAX or not nxt
    add(("second", NCH - 1), ("finish", 0))
    return out


EVENTS = {kind: events(kind) for kind in ("START", "BODY", "BODY_MID", "END")}
WORK = {kind: [x for what, x in ev if what == "work"] for kind, ev in EVENTS.items()}
SCORES = {kind: [e for e in ev if e[0] in ("score", "max")] for kind, ev in EVENTS.items()}


def uses(table, bank):
    return {kind: len(stages[bank::2]) for kind, stages in table.items()}


DVE_STEPS = {"START": 12, "BODY": 21, "BODY_MID": 27, "END": 9}


def program(nc, x_in, out, w):
    ctx = ExitStack()
    with ctx:
        def sb(name, shape, dt=F32):
            return ctx.enter_context(nc.sbuf_tensor(name, shape, dt))

        def sem(name):
            return ctx.enter_context(nc.semaphore(name))

        signals = []

        def signal(name, per):
            signals.append(Signal(sem(name), per))
            return signals[-1]

        between = nc.dram_tensor("between", [B, T, D], F32, kind="Internal").ap()
        q_stack_d = nc.dram_tensor("q_stack_d", [64 // HD, P, T], BF16, kind="Internal").ap()
        k_stack_d = nc.dram_tensor("k_stack_d", [64 // HD, P, T], BF16, kind="Internal").ap()
        nmax_d = nc.dram_tensor("nmax_d", [3 * NH, T], BF16, kind="Internal").ap()

        wq = sb("wq", [P, 2, P])
        wdkv = sb("wdkv", [P, LAT])
        wukv_raw = sb("wukv_raw", [LAT, 2 * P])
        lat_affine = sb("lat_affine", [LAT, P])
        wk = sb("wk", [P, 2, P])
        wv = sb("wv", [P, P])
        wo = sb("wo", [P, P])
        gate = sb("gate", [P, NE])
        gate_b = sb("gate_b", [P, NE])
        w1 = sb("w1", [P, NE * HID])
        w2 = sb("w2", [P, NCH, D])
        b1 = sb("b1", [P, NCH])
        b2 = sb("b2", [NE, D])
        relu_b1 = sb("relu_b1", [P, NCH])
        relu_b1_by_e = sb("relu_b1_by_e", [P, NCH, NE])
        idle_sum = sb("idle_sum", [P, 1])
        own_bias = sb("own_bias", [NE, D])
        n1w = sb("n1w", [P, 1])
        n2w = sb("n2w", [P, 1])
        lng = sb("lng", [LAT, 1])
        lnb = sb("lnb", [LAT, 1])
        cos = sb("cos", [P, T])
        sin = sb("sin", [P, T])
        ident = sb("ident", [P, P])
        ident_b = sb("ident_b", [P, P], BF16)
        mask_q = sb("mask_q", [P, P], BF16)
        mask_k = sb("mask_k", [P, P], BF16)
        sel_e = sb("sel_e", [NE, NE, P], BF16)
        rank = sb("rank", [P, NT, NE])
        half_pow = sb("half_pow", [P, 8])

        x = sb("x", [P, NT, D])
        u = sb("u", [P, NT, D + 1])
        n = sb("n", [P, NT, D])
        stats = sb("stats", [P, NT, 6])
        mv = sb("mv", [P, NT, 2])
        u_saved = sb("u_saved", [P, NT, D])
        recip_m = sb("recip_m", [P, NT])
        powin_b = sb("powin_b", [P, NT])
        powout_b = sb("powout_b", [P, NT])
        met = sb("met", [P, 1])
        zero = sb("zero", [P, 1])
        powin = sb("powin", [P, 8])
        powout = sb("powout", [P, 8])
        nT = sb("nT", [P, T])
        zn = sb("zn", [P, NT, P])
        znT = sb("znT", [P, T])
        rope_a = sb("rope_a", [P, 2, T])
        rope_b = sb("rope_b", [P, 2, T])
        qk = sb("qk", [P, 2, T])
        rest = sb("rest", [P, 2, T])
        parts = sb("parts", [P, 2, 3, T], BF16)
        qs = sb("qs", [P, NPAIR, T], BF16)
        kz = sb("kz", [P, 2, NPAIR, T], BF16)
        v = sb("v", [P, NT, NH, 32])
        nmax = sb("nmax", [P, NT, NH])
        nmax_rest = sb("nmax_rest", [P, NT, NH])
        nmax_parts = sb("nmax_parts", [P, NT, P], BF16)
        nmaxT = sb("nmaxT", [3 * NH, T], BF16)
        pT = sb("pT", [P, 2, 4, PCOLS])
        oT_raw = sb("oT_raw", [P, NG, T])
        recip = sb("recip", [P, NT, 4])
        o = sb("o", [P, NT, D])
        oT = sb("oT", [P, T])
        x2 = sb("x2", [P, NT, D])
        square = sb("square", [P, NT, D])
        n2 = sb("n2", [P, NT, D])
        n2T = sb("n2T", [P, T])
        base = sb("base", [P, NT, D])
        base_next = sb("base_next", [P, NT, D])
        logit = sb("logit", [P, NT, NE])
        top = sb("top", [P, NT])
        onehot = sb("onehot", [P, NT, NE])
        ohT = sb("ohT", [NE, T])
        ohT_b = sb("ohT_b", [NE, T], BF16)
        xe = sb("xe", [P, NE, T])
        hid = sb("hid", [P, 4, T])
        yT = sb("yT", [P, T])
        res = sb("res", [P, NT, D])
        rnorm = sb("rnorm", [P, NT])
        rnorm_w = sb("rnorm_w", [P, NT, P])
        rrow = sb("rrow", [P, T])
        sim = xe
        esim = hid

        SC = [ctx.enter_context(nc.psum_tensor(f"score{i}", [P, 2, 512], F32)) for i in range(2)]
        W = [ctx.enter_context(nc.psum_tensor(f"work{i}", [P, 512], F32)) for i in range(2)]
        A = [ctx.enter_context(nc.psum_tensor(f"accum{i}", [P, 512], F32)) for i in range(2)]

        loads = sem("loads")
        ones_loaded = sem("ones_loaded")
        setup_pe = sem("setup_pe")
        setup_dve = sem("setup_dve")
        setup_pool = sem("setup_pool")
        padded = sem("padded")
        x_loaded = signal("x_loaded", ("front", 16))
        x_read = signal("x_read", ("front", 1))
        pow_in = signal("pow_in", ("front", 2))
        pow_out = signal("pow_out", ("front", 2))
        mid_pow_in = signal("mid_pow_in", ("mid", 2))
        mid_pow_out = signal("mid_pow_out", ("mid", 2))
        back_pow_in = signal("back_pow_in", ("back", 1))
        back_pow_out = signal("back_pow_out", ("back", 1))
        dve_step = signal("dve_step", DVE_STEPS)
        pool_step = signal("pool_step", ("front", 3))
        n_ready = signal("n_ready", ("front", 1))
        mid_u_ready = signal("mid_u_ready", ("mid", 1))
        q_ready = signal("q_ready", ("front", 1))
        parts_ready = [signal(f"parts_ready{s}", ("front", 1)) for s in "qk"]
        stack_stored = [signal(f"{s}_stack_stored", ("front", 16 * len(SLOTS))) for s in "qk"]
        stack_loaded = [signal(f"stack_loaded{i}", ("front", 16 * 4)) for i in range(2)]
        nmax_ready = signal("nmax_ready", ("front", 1))
        nmax_stored = signal("nmax_stored", ("front", 16))
        nmax_loaded = signal("nmax_loaded", ("front", 32))
        sc_full = [signal(f"sc_full{i}", uses(SCORES, i)) for i in range(2)]
        sc_free = [signal(f"sc_free{i}", uses(SCORES, i)) for i in range(2)]
        w_full = [signal(f"w_full{i}", uses(WORK, i)) for i in range(2)]
        w_free = [signal(f"w_free{i}", uses(WORK, i)) for i in range(2)]
        a_full = [signal(f"a_full{i}", ("back", 3 - i)) for i in range(2)]
        a_free = [signal(f"a_free{i}", ("back", 2)) for i in range(2)]
        n2_ready = signal("n2_ready", ("back", 1))
        onehot_ready = signal("onehot_ready", ("back", 1))
        y_step = signal("y_step", ("back", NCH))
        yT_ready = signal("yT_ready", ("back", 1))
        res_ready = signal("res_ready", ("back", 1))
        out_stored = signal("out_stored", ("back", 16))
        rnorm_ready = signal("rnorm_ready", ("mid", 1))
        exp_ready = signal("exp_ready", ("mid", NT))
        x_new = signal("x_new", ("mid", 1))
        setup_steps = sem("setup_steps")

        block = ctx.enter_context(nc.Block())

        def work(body, name):
            k = WORK[body.kind].index(name)
            return k % 2, k // 2 + 1

        def filled(body, name):
            i, k = work(body, name)
            return w_full[i].at(body, k)

        def read_out(body, name):
            i, k = work(body, name)
            return w_free[i].at(body, k)

        def bank_of(body, name):
            return work(body, name)[0]

        def scores(body, what, unit):
            k = SCORES[body.kind].index((what, unit))
            return k % 2, k // 2 + 1

        def bodies(eng, run):
            run(Body("START"))
            with eng.Fori(0, B - 1) as b:
                run(Body("BODY", b))
            with eng.Fori(0, B) as b:
                run(Body("BODY_MID", b))
            run(Body("END"))

        @block.sync
        def _(sp):
            for s in signals:
                sp.sem_inc(s.sem, 1)
            sp.dma_start(x[:, :, :], x_in[0].rearrange("(t p) d -> p t d", p=P)).then_inc(x_loaded.sem, 16)
            for dst, src in ((wq[:, 0, :], w["WqT"]), (wdkv[:, :], w["WdkvT"]), (wukv_raw[:, 0:P], w["WukT"]),
                             (wukv_raw[:, P:], w["WuvT"]), (wo[:, :], w["WoT"]), (gate[:, :], w["gateT"]),
                             (gate_b[:, :], w["gate_b"].to_broadcast([P, NE])), (b1[:, :], w["b1T"]),
                             (b2[:, :], w["b2"]), (n1w[:, :], w["n1"]), (n2w[:, :], w["n2"]), (lng[:, :], w["ln_g"]),
                             (lnb[:, :], w["ln_b"]), (cos[:, :], w["cos"]), (sin[:, :], w["sin"]),
                             (w1[:, :], w["W1T"]), (w2[:, :, :], w["W2T"])):
                sp.dma_start(dst, src).then_inc(loads, 16)
            for stack, pad in ((q_stack_d, "pad_q"), (k_stack_d, "pad_k")):
                sp.dma_start(stack[N_SLOT:, :, :], w[pad]).then_inc(padded, 16)

            def load_x(src):
                sp.dma_start(x[:, :, :], src.rearrange("(t p) d -> p t d", p=P)).then_inc(x_loaded.sem, 16)

            def store_stacks(body):
                for s, stack in enumerate((q_stack_d, k_stack_d)):
                    sp.wait_ge(*parts_ready[s].at(body, 1))
                    for first, n, part in SLOTS:
                        src = parts[:, 1, 0:n, :] if s else parts[:, 0, part:part + 1, :].to_broadcast([P, n, T])
                        sp.dma_start(stack[first:first + n].rearrange("s m n -> m s n"), src)\
                          .then_inc(stack_stored[s].sem, 16)
                    if s == 0:
                        load_q(body, 0)

            def rows_of(stack, j, half):
                return stack.rearrange("s (d j p) n -> j (s d) p n", d=HD, j=2)[j, :, NHALF * half:NHALF * (half + 1)]

            def load_q(body, half):
                if body.kind != "START":
                    for i in range(2):
                        unit = [u for u in range(N_SCORE * (half + 1) // 2) if scores(body, "score", u)[0] == i][-1]
                        sp.wait_ge(*sc_full[i].at(body, scores(body, "score", unit)[1]))
                if half == 0:
                    sp.wait_ge(*stack_stored[0].at(body, stack_stored[0].per[1]))
                for j in range(2):
                    sp.dma_start(qs[64 * j:64 * j + 64, NHALF * half:NHALF * (half + 1), :], rows_of(q_stack_d, j, half))\
                      .then_inc(stack_loaded[half].sem, 16)

            def load_k(half):
                for j in range(2):
                    sp.dma_start(kz[64 * j:64 * j + 64, j, NHALF * half:NHALF * (half + 1), :],
                                 rows_of(k_stack_d, j, half)).then_inc(stack_loaded[half].sem, 16)

            def load_nmax(body):
                sp.wait_ge(*read_out(body, "T_NMAX"))
                sp.dma_start(nmax_d, nmaxT[:, :]).then_inc(nmax_stored.sem, 16)
                sp.wait_ge(*nmax_stored.at(body, 16))
                for j in range(2):
                    r = 64 * j + MAXROW
                    sp.dma_start(qs[r:r + 3, :, :], nmax_d.rearrange("(s p j) n -> j s p n", s=3, j=2)[j])\
                      .then_inc(nmax_loaded.sem, 16)

            def store_result(body, dst):
                sp.wait_ge(*res_ready.at(body, 1))
                sp.dma_start(dst.rearrange("(t p) d -> p t d", p=P), res[:, :, :]).then_inc(out_stored.sem, 16)

            def front(body, x_next):
                if x_next is not None:
                    sp.wait_ge(*x_read.at(body, 1))
                    load_x(x_next)
                store_stacks(body)
                sp.wait_ge(*stack_stored[1].at(body, stack_stored[1].per[1]))
                load_k(0)
                load_q(body, 1)
                load_k(1)
                load_nmax(body)

            def beside(body, dst, x_next):
                front(body, x_next)
                store_result(body, dst)

            sp.wait_ge(setup_pool, 1)
            sp.wait_ge(padded, 32)
            front(Body("START"), x_in[1])
            with sp.Fori(0, B - 2) as b:
                beside(Body("BODY", b), between[b], x_in[b + 2])
            sp.wait_ge(out_stored.sem, 16 * (B - 2) + 1)
            beside(Body("BODY", B - 2), between[B - 2], between[0])
            beside(Body("BODY_MID", 0), between[B - 1], between[1])
            sp.wait_ge(out_stored.sem, 16 * B + 1)
            with sp.Fori(1, B - 1) as b:
                beside(Body("BODY_MID", b), out[b - 1], between[b + 1])
            beside(Body("BODY_MID", B - 1), out[B - 2], None)
            store_result(Body("END"), out[B - 1])
            sp.wait_ge(out_stored.sem, 2 * 16 * B + 1)

        @block.gpsimd
        def _(pool):
            pool.memset(kz[:, :, :, :], 0.0)
            pool.memset(zero[:, :], 0.0)
            pool.memset(nmax_parts[:, :, :], 0.0)
            pool.memset(half_pow[:, :], -0.5)
            pool.memset(ident[:, :], 0.0)
            pool.memset(ident_b[:, :], 0.0)
            pool.memset(mask_q[:, :], 0.0)
            pool.memset(mask_k[:, :], 0.0)
            pool.memset(sel_e[:, :, :], 0.0)
            pool.memset(lat_affine[:, :], 0.0)
            pool.memset(zn[:, :, :], 0.0)
            pool.memset(v[:, :, :, :], 0.0)
            for e in range(NE):
                pool.memset(rank[:, :, e:e + 1], float(NE - e))
            pool.memset(relu_b1_by_e[:, :, :], 0.0)
            pool.memset(u[:, :, D:D + 1], 1.0).then_inc(setup_pool, 1)
            pool.wait_ge(setup_pool, 1)
            pool.memset(zn[:, :, LAT:LAT + 1], 1.0)
            pool.memset(v[:, :, :, HD:HD + 1], 1.0)
            for m in (ident, ident_b):
                pool.affine_select(out=m[:, :], in_=m[:, :], compare_op=ALU.not_equal, fill=1.0, base=0,
                                   pattern=[[-1, P]], channel_multiplier=1)
            pool.affine_select(out=mask_q[:, :], in_=mask_q[:, :], compare_op=ALU.is_ge, fill=MASKED, base=0,
                               pattern=[[-1, P]], channel_multiplier=1)
            pool.affine_select(out=mask_k[:, :], in_=mask_k[:, :], compare_op=ALU.is_ge, fill=MASKED, base=0,
                               pattern=[[1, P]], channel_multiplier=-1)
            pool.affine_select(out=sel_e[:, :, :], in_=sel_e[:, :, :], compare_op=ALU.not_equal, fill=1.0, base=0,
                               pattern=[[-1, NE], [0, P]], channel_multiplier=1).then_inc(setup_pool, 1)

            def power(body, asked, given, k, dst, src, cols):
                pool.wait_ge(*asked.at(body, k))
                pool.tensor_tensor(dst[:, 0:cols], src[:, 0:cols], half_pow[:, 0:cols], ALU.pow).then_inc(given.sem, 1)

            def split_q(body):
                zeros = zero[:, 0:1].to_broadcast([P, T])
                pool.wait_ge(*stack_stored[0].at(body, 0))
                pool.wait_ge(*q_ready.at(body, 1))
                pool.tensor_tensor(parts[:, 0, 0, :], qk[:, 0, :], zeros, ALU.add).then_inc(pool_step.sem, 1)
                pool.wait_ge(*pool_step.at(body, 1))
                pool.tensor_tensor(rest[:, 0, :], qk[:, 0, :], parts[:, 0, 0, :], ALU.subtract).then_inc(pool_step.sem, 1)
                pool.wait_ge(*pool_step.at(body, 2))
                pool.tensor_tensor(parts[:, 0, 1, :], rest[:, 0, :], zeros, ALU.add).then_inc(pool_step.sem, 1)
                pool.wait_ge(*pool_step.at(body, 3))
                pool.tensor_tensor(parts[:, 0, 2, :], rest[:, 0, :], parts[:, 0, 1, :], ALU.subtract)\
                    .then_inc(parts_ready[0].sem, 1)

            def run(body):
                if body.kind == "BODY_MID":
                    power(body, mid_pow_in, mid_pow_out, 1, powout, powin, 4)
                    power(body, mid_pow_in, mid_pow_out, 2, powout, powin, 4)
                if body.kind != "END":
                    power(body, pow_in, pow_out, 1, powout, powin, 8)
                    power(body, pow_in, pow_out, 2, powout, powin, 4)
                    split_q(body)
                if body.kind != "START":
                    power(body, back_pow_in, back_pow_out, 1, powout_b, powin_b, 4)

            bodies(pool, run)

        @block.scalar
        def _(act):
            def copy(body, name, dst, src):
                i = bank_of(body, name)
                act.wait_ge(*filled(body, name))
                nc.scalar.activation(dst, src(W[i]), ACT.Copy).then_inc(w_free[i].sem, 1)

            def whole(bank):
                return bank[:, :]

            def exponential(body, unit):
                p, z = unit // 3, unit % 3
                g, half = p // 2, 2 * (p % 2)
                if unit % 6 == 0:
                    act.wait_ge(*a_full[g % 2].at(body, g // 2))
                i, k = scores(body, "score", unit)
                act.wait_ge(*sc_full[i].at(body, k))
                if z < 2:
                    ins = nc.scalar.activation(pT[:, g % 2, half + z, 0:1024],
                                               SC[i][:, :, :].rearrange("p a n -> p (a n)"), ACT.Exp, scale=SCALE)
                else:
                    ins = nc.scalar.activation(pT[:, g % 2, half:half + 2, 1024:PCOLS],
                                               SC[i][:, 0, :].rearrange("p (j n) -> p j n", j=2),
                                               ACT.Exp, scale=SCALE)
                ins.then_inc(sc_free[i].sem, 1)

            def run(body):
                for what, k in EVENTS[body.kind]:
                    if what == "score":
                        exponential(body, k)
                    elif what != "work":
                        continue
                    elif k == "T_U":
                        copy(body, k, nT[:, :], whole)
                    elif k == "RROW":
                        copy(body, k, rrow[:, :], whole)
                    elif k.startswith("DOTS"):
                        t = int(k[4:])
                        act.wait_ge(*read_out(body, k))
                        nc.scalar.activation(esim[:, t, :], sim[:, t, :], ACT.Exp).then_inc(exp_ready.sem, 1)
                    elif k == "T_N":
                        copy(body, k, nT[:, :], whole)
                    elif k == "T_Z":
                        copy(body, k, znT[:, :], whole)
                    elif k == "V":
                        if body.kind != "START":
                            act.wait_ge(*a_full[1].at(body, 2))
                        copy(body, k, v[:, :, :, 0:HD],
                             lambda bank: bank[:, :].rearrange("p (t h d) -> p t h d", t=NT, d=HD))
                    elif k == "T_NMAX":
                        copy(body, k, nmaxT[:, :], lambda bank: bank[0:3 * NH, :].bitcast(BF16)[:, 0:T])
                    elif k == "T_O":
                        copy(body, k, oT[:, :], whole)
                    elif k == "T_N2":
                        copy(body, k, n2T[:, :], whole)
                    elif k == "T_OH":
                        i = bank_of(body, k)
                        act.wait_ge(*filled(body, k))
                        nc.scalar.activation(ohT[:, :], W[i][0:NE, :], ACT.Copy)
                        nc.scalar.activation(ohT_b[:, :], W[i][0:NE, :], ACT.Copy).then_inc(w_free[i].sem, 1)
                    elif k.startswith("HIDDEN"):
                        c = int(k[6:])
                        i = bank_of(body, k)
                        act.wait_ge(*filled(body, k))
                        if c >= 4:
                            act.wait_ge(*y_step.at(body, c - 3))
                        nc.scalar.activation(hid[:, c % 4, :], W[i][:, :], ACT.Relu, bias=b1[:, c:c + 1])\
                            .then_inc(w_free[i].sem, 1)

            act.wait_ge(loads, 16 * 17)
            bodies(act, run)

        @block.tensor
        def _(pe):
            pe.wait_ge(setup_dve, 1)
            pe.matmul(W[0][:, 0:2 * P], lat_affine[:, :], wukv_raw[:, :], start=True, stop=True).then_inc(setup_pe, 1)
            for c in range(NCH):
                pe.matmul(W[1][:, 0:1], w2[:, c, :], relu_b1[:, c:c + 1], start=(c == 0), stop=(c == NCH - 1))
            for c in range(NCH):
                last = pe.matmul(A[0][0:NE, 0:D], relu_b1_by_e[:, c, :], w2[:, c, :],
                                 start=(c == 0), stop=(c == NCH - 1))
            last.then_inc(setup_pe, 1)
            pe.wait_ge(setup_dve, 2)

            def transposes(src, rows=P):
                def emit(bank):
                    for t in range(NT):
                        last = pe.transpose(bank[0:rows, t * P:(t + 1) * P], src(t), ident[:, :])
                    return last
                return emit

            def product(lhsT, rhs):
                return lambda bank: pe.matmul(bank[:, :], lhsT, rhs, start=True, stop=True)

            def by_token(src, weight, cols):
                def emit(bank):
                    for t in range(NT):
                        last = pe.matmul(bank[:, t * cols:(t + 1) * cols], src[:, t * P:(t + 1) * P], weight,
                                         start=True, stop=True)
                    return last
                return emit

            def turn_max(bank):
                for t in range(NT):
                    last = pe.transpose(bank[:, :].bitcast(BF16)[:, t * P:(t + 1) * P], nmax_parts[:, t, :],
                                        ident_b[:, :])
                return last

            def norm_rows(bank):
                for t in range(NT):
                    last = pe.matmul(bank[:, t * P:(t + 1) * P], rnorm_w[:, t, :], ident[:, :], start=True, stop=True)
                return last

            def attend(a):
                def emit(bank):
                    for i in range(2):
                        q0 = (2 * a + i) * P
                        for t in range(NT):
                            last = pe.matmul(bank[:, i * (D + 1):(i + 1) * (D + 1)], esim[:, t, q0:q0 + P], u[:, t, :],
                                             start=(t == 0), stop=(t == NT - 1))
                    return last
                return emit

            def stage(body, name):
                if name == "T_U":
                    pe.wait_ge(*mid_u_ready.at(body, 1))
                    return transposes(lambda t: u[:, t, 0:D])
                if name == "RROW":
                    pe.wait_ge(*rnorm_ready.at(body, 1))
                    return norm_rows
                if name.startswith("DOTS"):
                    t = int(name[4:])
                    if t == 0:
                        pe.wait_ge(*read_out(body, "T_U"))
                    return product(nT[:, t * P:(t + 1) * P], nT[:, :])
                if name.startswith("AV"):
                    pe.wait_ge(*exp_ready.at(body, NT))
                    return attend(int(name[2:]))
                if name == "T_N":
                    pe.wait_ge(*n_ready.at(body, 1))
                    return transposes(lambda t: n[:, t, :])
                if name == "LATENT":
                    pe.wait_ge(*read_out(body, "T_N"))
                    return by_token(nT, wdkv[:, :], LAT)
                if name in ("Q", "QR"):
                    return product(wq[:, ("Q", "QR").index(name), :], nT[:, :])
                if name == "T_Z":
                    pe.wait_ge(*read_out(body, "LATENT"))
                    return transposes(lambda t: zn[:, t, :])
                if name in ("K", "KR"):
                    pe.wait_ge(*read_out(body, "T_Z"))
                    return product(wk[:, ("K", "KR").index(name), :], znT[:, :])
                if name == "V":
                    return by_token(znT, wv[:, :], P)
                if name == "T_NMAX":
                    pe.wait_ge(*nmax_ready.at(body, 1))
                    return turn_max
                if name.startswith("T_OUT"):
                    g = int(name[5:])
                    pe.wait_ge(*a_free[g % 2].at(body, g // 2 + 1))
                    return transposes(lambda t: oT_raw[:, g, t * P:(t + 1) * P])
                if name == "T_O":
                    pe.wait_ge(*read_out(body, f"T_OUT{NG - 1}"))
                    return transposes(lambda t: o[:, t, :])
                if name == "WO":
                    pe.wait_ge(*read_out(body, "T_O"))
                    return by_token(oT, wo[:, :], D)
                if name == "T_N2":
                    pe.wait_ge(*n2_ready.at(body, 1))
                    return transposes(lambda t: n2[:, t, :])
                if name == "LOGIT":
                    pe.wait_ge(*read_out(body, "T_N2"))
                    return by_token(n2T, gate[:, :], NE)
                if name == "T_OH":
                    pe.wait_ge(*onehot_ready.at(body, 1))
                    return transposes(lambda t: onehot[:, t, :], NE)
                if name.startswith("MASK"):
                    pe.wait_ge(*read_out(body, "T_OH"))
                    return product(sel_e[:, int(name[4:]), :], ohT_b[:, :])
                c = int(name[6:])
                pe.wait_ge(*read_out(body, f"MASK{c // NC}"))
                return product(w1[:, c * P:(c + 1) * P], xe[:, c // NC, :])

            def max_unit(body, unit):
                p, qt = unit // NT, unit % NT
                cols = (qt + 1) * P
                if unit in (0, N_MAX // 2):
                    half = unit // (N_MAX // 2)
                    pe.wait_ge(*stack_loaded[half].at(body, stack_loaded[half].per[1]))
                i, k = scores(body, "max", unit)
                pe.wait_ge(*sc_free[i].at(body, k - 1))
                for j in range(2):
                    pe.matmul(SC[i][:, j, 0:cols], qs[:, p, qt * P:(qt + 1) * P], kz[:, j, p, 0:cols],
                              start=True, stop=False)
                    last = pe.matmul(SC[i][:, j, cols - P:cols], ident_b[:, :], mask_q[:, :], start=False, stop=True)
                last.then_inc(sc_full[i].sem, 1)

            def key_tile(bank, at, p, h, kt):
                q0 = kt * P
                pe.matmul(bank[:, at:at + T - q0], kz[:, h % 2, p, q0:q0 + P], qs[:, p, q0:T], start=True, stop=False)
                return pe.matmul(bank[:, at:at + P], ident_b[:, :], mask_k[:, :], start=False, stop=True)

            def score_unit(body, unit):
                p, z = unit // 3, unit % 3
                i, k = scores(body, "score", unit)
                pe.wait_ge(*sc_free[i].at(body, k - 1))
                if z < 2:
                    h = 2 * p + z
                    key_tile(SC[i][:, 0], 0, p, h, 0)
                    key_tile(SC[i][:, 1], 0, p, h, 1)
                    last = key_tile(SC[i][:, 1], 384, p, h, 3)
                else:
                    key_tile(SC[i][:, 0], 0, p, 2 * p, 2)
                    last = key_tile(SC[i][:, 0], 256, p, 2 * p + 1, 2)
                last.then_inc(sc_full[i].sem, 1)

            def weighted_sum(body, g):
                a = g % 2
                for i in range(2):
                    unit = [q for q in range(6 * g, 6 * g + 6) if scores(body, "score", q)[0] == i][-1]
                    pe.wait_ge(*sc_free[i].at(body, scores(body, "score", unit)[1]))
                if g < 2:
                    pe.wait_ge(*(res_ready, yT_ready)[g].at(body, 0))
                else:
                    pe.wait_ge(*a_free[a].at(body, 1))
                for i, (kt, (at, q0)) in enumerate(KT_AT.items()):
                    for j in range(4):
                        last = pe.matmul(A[a][32 * j:32 * j + 32, q0:T], v[:, kt, 4 * g + j, :],
                                         pT[:, a, j, at:at + T - q0], start=(i == 0), stop=(i == NT - 1))
                last.then_inc(a_full[a].sem, 1)

            def second(body, c):
                if c == 0:
                    pe.wait_ge(*a_free[1].at(body, 2))
                    pe.matmul(A[1][:, :], own_bias[:, :], ohT[:, :], start=True, stop=False)
                pe.wait_ge(*read_out(body, f"HIDDEN{c}"))
                pe.matmul(A[1][:, :], w2[:, c, :], hid[:, c % 4, :], start=False, stop=(c == NCH - 1))\
                    .then_inc(y_step.sem, 1)

            def run(body):
                for what, k in EVENTS[body.kind]:
                    if what == "work":
                        emit = stage(body, k)
                        i, uses_so_far = work(body, k)
                        pe.wait_ge(*w_free[i].at(body, uses_so_far - 1))
                        emit(W[i]).then_inc(w_full[i].sem, 1)
                    elif what == "score":
                        if k == 0:
                            pe.wait_ge(*nmax_loaded.at_end_of(body.item("back")))
                        score_unit(body, k)
                    elif what == "sum":
                        weighted_sum(body, k)
                    elif what == "max":
                        max_unit(body, k)
                    elif what == "second":
                        second(body, k)
                    elif what == "finish":
                        pe.wait_ge(*yT_ready.at(body, 1))
                        pe.wait_ge(*a_free[0].at(body, 2))
                        for t in range(NT):
                            last = pe.transpose(A[0][:, t * P:(t + 1) * P], yT[:, t * P:(t + 1) * P], ident[:, :])
                        last.then_inc(a_full[0].sem, 1)

            bodies(pe, run)

        @block.vector
        def _(dve):
            V_ = nc.vector
            counted = {}

            def then(body, ins):
                ins.then_inc(dve_step.sem, 1)
                counted[body.kind] = counted.get(body.kind, 0) + 1
                dve.wait_ge(*dve_step.at(body, counted[body.kind]))

            dve.wait_ge(loads, 16 * 17)
            dve.wait_ge(setup_pool, 2)
            V_.tensor_scalar(lat_affine[:, 0:LAT], ident[0:LAT, 0:LAT], lng[:, 0:1], None, ALU.mult)
            V_.tensor_copy(lat_affine[:, LAT:LAT + 1], lnb[:, :])
            V_.tensor_scalar(wq[:, 0, :], wq[:, 0, :], n1w[:, 0:1], None, ALU.mult)
            V_.tensor_scalar(wdkv[:, :], wdkv[:, :], n1w[:, 0:1], None, ALU.mult)
            V_.tensor_scalar(gate[:, :], gate[:, :], n2w[:, 0:1], None, ALU.mult)
            V_.tensor_scalar(w1[:, :], w1[:, :], n2w[:, 0:1], None, ALU.mult)
            V_.tensor_scalar(relu_b1[:, :], b1[:, :], 0.0, None, ALU.max).then_inc(setup_steps, 1)
            dve.wait_ge(setup_steps, 1)
            for e in range(NE):
                last = V_.tensor_copy(relu_b1_by_e[:, e * NC:(e + 1) * NC, e:e + 1],
                                      relu_b1[:, e * NC:(e + 1) * NC].rearrange("p (c o) -> p c o", o=1))
            last.then_inc(setup_dve, 1)
            dve.wait_ge(setup_pe, 1)
            V_.tensor_copy(wk[:, 0, :], W[0][:, 0:P])
            V_.tensor_copy(wv[:, :], W[0][:, P:2 * P]).then_inc(setup_steps, 1)
            dve.wait_ge(setup_steps, 2)
            for m in (wq, wk):
                V_.tensor_scalar(m[:, 1, 0:P // 2], m[:, 0, P // 2:P], -1.0, None, ALU.mult)
                V_.tensor_copy(m[:, 1, P // 2:P], m[:, 0, 0:P // 2])
            dve.wait_ge(setup_pe, 2)
            V_.tensor_copy(idle_sum[:, :], W[1][:, 0:1])
            V_.tensor_tensor(own_bias[:, :], A[0][0:NE, 0:D], b2[:, :], ALU.add).then_inc(setup_dve, 1)
            dve.wait_ge(setup_dve, 2)

            def moments(body, src):
                for t in range(NT):
                    ins = V_.bn_stats(stats[:, t, :], src(t))
                then(body, ins)
                V_.tensor_copy(met[:, :], stats[:, 0, 0:1])
                for t in range(NT):
                    ins = V_.bn_aggr(mv[:, t, :], stats[:, t, :])
                then(body, ins)

            def normed(dst, factor):
                for t in range(NT):
                    ins = V_.tensor_scalar(dst[:, t, 0:D], x[:, t, :], mv[:, t, 0:1], factor[:, t:t + 1],
                                           ALU.subtract, ALU.mult)
                return ins

            def front(body):
                if body.kind == "BODY_MID":
                    dve.wait_ge(*x_new.at(body, 1))
                else:
                    dve.wait_ge(*x_loaded.at(body, 16))
                moments(body, lambda t: x[:, t, :])
                V_.tensor_scalar(powin[:, 4:8], mv[:, :, 1], 1.0 + RMS_EPS, RMS_EPS * LN_EPS, ALU.mult, ALU.add)
                V_.tensor_scalar(powin[:, 0:4], mv[:, :, 1], LN_EPS, None, ALU.add).then_inc(pow_in.sem, 1)
                dve.wait_ge(*pow_out.at(body, 1))
                normed(n, powout[:, 4:8]).then_inc(n_ready.sem, 1)
                then(body, normed(u, powout[:, 0:4]))
                V_.scalar_tensor_tensor(out=base_next[:, :, :], in0=u[:, :, 0:D], scalar=0.5, in1=x[:, :, :],
                                        op0=ALU.mult, op1=ALU.add).then_inc(x_read.sem, 1)

            def latent(body):
                i = bank_of(body, "LATENT")
                dve.wait_ge(*filled(body, "LATENT"))
                lat = W[i][:, 0:NT * LAT].rearrange("p (t c) -> p t c", t=NT)
                moments(body, lambda t: lat[:, t, :])
                V_.tensor_scalar(powin[:, 0:4], mv[:, :, 1], LN_EPS, None, ALU.add).then_inc(pow_in.sem, 1)
                dve.wait_ge(*pow_out.at(body, 2))
                for t in range(NT):
                    ins = V_.tensor_scalar(zn[:, t, 0:LAT], lat[:, t, :], mv[:, t, 0:1], powout[:, t:t + 1],
                                           ALU.subtract, ALU.mult)
                ins.then_inc(w_free[i].sem, 1)

            def rope(body, name):
                s = "QK".index(name[0])
                i = bank_of(body, name)
                dve.wait_ge(*filled(body, name))
                if name in "QK":
                    V_.tensor_tensor(rope_a[:, s, :], W[i][:, :], cos[:, :], ALU.mult).then_inc(w_free[i].sem, 1)
                    return
                V_.tensor_tensor(rope_b[:, s, :], W[i][:, :], sin[:, :], ALU.mult).then_inc(w_free[i].sem, 1)
                dve.wait_ge(*read_out(body, name[0]))
                dve.wait_ge(*read_out(body, name))
                if name == "QR":
                    dve.wait_ge(*parts_ready[0].at(body, 0))
                    V_.tensor_tensor(qk[:, s, :], rope_a[:, s, :], rope_b[:, s, :], ALU.add).then_inc(q_ready.sem, 1)
                    return
                then(body, V_.tensor_tensor(qk[:, s, :], rope_a[:, s, :], rope_b[:, s, :], ALU.add))
                dve.wait_ge(*stack_stored[1].at(body, 0))
                then(body, V_.tensor_copy(parts[:, s, 0, :], qk[:, s, :]))
                then(body, V_.tensor_tensor(rest[:, s, :], qk[:, s, :], parts[:, s, 0, :], ALU.subtract))
                then(body, V_.tensor_copy(parts[:, s, 1, :], rest[:, s, :]))
                V_.tensor_tensor(parts[:, s, 2, :], rest[:, s, :], parts[:, s, 1, :], ALU.subtract)\
                  .then_inc(parts_ready[1].sem, 1)

            def row_max(body, unit):
                p, qt = unit // NT, unit % NT
                i, k = scores(body, "max", unit)
                dve.wait_ge(*sc_full[i].at(body, k))
                V_.tensor_reduce(nmax[:, qt, 2 * p:2 * p + 2], SC[i][:, :, 0:(qt + 1) * P], AX.X, ALU.max,
                                 negate=True).then_inc(sc_free[i].sem, 1)

            def split_max(body):
                for i in range(2):
                    unit = [m for m in range(N_MAX) if scores(body, "max", m)[0] == i][-1]
                    dve.wait_ge(*sc_free[i].at(body, scores(body, "max", unit)[1]))
                then(body, V_.tensor_copy(nmax_parts[:, :, 0:NH], nmax[:, :, :]))
                then(body, V_.tensor_tensor(nmax_rest[:, :, :], nmax[:, :, :], nmax_parts[:, :, 0:NH], ALU.subtract))
                then(body, V_.tensor_copy(nmax_parts[:, :, NH:2 * NH], nmax_rest[:, :, :]))
                V_.tensor_tensor(nmax_parts[:, :, 2 * NH:3 * NH], nmax_rest[:, :, :], nmax_parts[:, :, NH:2 * NH],
                                 ALU.subtract).then_inc(nmax_ready.sem, 1)

            def out_copy(body, g):
                dve.wait_ge(*a_full[g % 2].at(body, g // 2 + 1))
                V_.tensor_copy(oT_raw[:, g, :], A[g % 2][:, :]).then_inc(a_free[g % 2].sem, 1)

            def divide(body, g):
                i = bank_of(body, f"T_OUT{g}")
                dve.wait_ge(*filled(body, f"T_OUT{g}"))
                bank = W[i][:, :].rearrange("p (t j c) -> p t j c", t=NT, c=32)
                then(body, V_.reciprocal(recip[:, :, :], bank[:, :, :, HD]))
                V_.tensor_tensor(o[:, :, 4 * HD * g:4 * HD * (g + 1)].rearrange("p t (j d) -> p t j d", d=HD),
                                 bank[:, :, :, 0:HD], recip[:, :, :].unsqueeze(3).to_broadcast([P, NT, 4, HD]),
                                 ALU.mult).then_inc(w_free[i].sem, 1)

            def residual(body):
                i = bank_of(body, "WO")
                dve.wait_ge(*filled(body, "WO"))
                attn = W[i][:, :].rearrange("p (t d) -> p t d", t=NT)
                then(body, V_.tensor_tensor(x2[:, :, :], attn, u_saved[:, :, :], ALU.add))
                V_.scalar_tensor_tensor(out=base[:, :, :], in0=attn, scalar=0.5, in1=base[:, :, :],
                                        op0=ALU.mult, op1=ALU.add).then_inc(w_free[i].sem, 1)
                for t in range(NT):
                    ins = V_.tensor_tensor_reduce(square[:, t, :], x2[:, t, :], x2[:, t, :], 1.0 / D, RMS_EPS,
                                                  ALU.mult, ALU.add, powin_b[:, t:t + 1])
                ins.then_inc(back_pow_in.sem, 1)

            def norm2(body):
                dve.wait_ge(*back_pow_out.at(body, 1))
                for t in range(NT):
                    ins = V_.tensor_scalar(n2[:, t, :], x2[:, t, :], powout_b[:, t:t + 1], None, ALU.mult)
                ins.then_inc(n2_ready.sem, 1)

            def choose(body):
                i = bank_of(body, "LOGIT")
                dve.wait_ge(*filled(body, "LOGIT"))
                V_.tensor_tensor(logit[:, :, :], W[i][:, 0:NT * NE].rearrange("p (t e) -> p t e", t=NT),
                                 gate_b[:, :].unsqueeze(1).to_broadcast([P, NT, NE]), ALU.add)\
                    .then_inc(w_free[i].sem, 1)
                dve.wait_ge(*read_out(body, "LOGIT"))
                for last in (False, True):
                    then(body, V_.tensor_reduce(top[:, :], logit[:, :, :], AX.X, ALU.max))
                    ins = V_.tensor_tensor(onehot[:, :, :], logit[:, :, :],
                                           top[:, :].unsqueeze(2).to_broadcast([P, NT, NE]), ALU.is_equal)
                    if last:
                        ins.then_inc(onehot_ready.sem, 1)
                    else:
                        then(body, ins)
                        then(body, V_.tensor_tensor(logit[:, :, :], onehot[:, :, :], rank[:, :, :], ALU.mult))

            def mask(body, e):
                i = bank_of(body, f"MASK{e}")
                dve.wait_ge(*filled(body, f"MASK{e}"))
                V_.tensor_tensor(xe[:, e, :], n2T[:, :], W[i][:, :], ALU.mult).then_inc(w_free[i].sem, 1)

            def finish(body):
                dve.wait_ge(*y_step.at(body, NCH))
                V_.tensor_scalar(yT[:, :], A[1][:, :], idle_sum[:, 0:1], None, ALU.subtract).then_inc(yT_ready.sem, 1)
                dve.wait_ge(*a_full[0].at(body, 3))
                dve.wait_ge(*out_stored.at(body, 0))
                V_.scalar_tensor_tensor(out=res[:, :, :], in0=A[0][:, :].rearrange("p (t d) -> p t d", t=NT), scalar=0.5,
                                        in1=base[:, :, :], op0=ALU.mult, op1=ALU.add).then_inc(res_ready.sem, 1)

            def save(body):
                dve.wait_ge(*res_ready.at(body, 0))
                V_.tensor_copy(u_saved[:, :, :], u[:, :, 0:D])
                V_.tensor_copy(base[:, :, :], base_next[:, :, :])

            def mid(body):
                dve.wait_ge(*x_loaded.at(body, 16))
                moments(body, lambda t: x[:, t, :])
                V_.tensor_scalar(powin[:, 0:4], mv[:, :, 1], LN_EPS, None, ALU.add).then_inc(mid_pow_in.sem, 1)
                dve.wait_ge(*mid_pow_out.at(body, 1))
                normed(u, powout[:, 0:4]).then_inc(mid_u_ready.sem, 1)
                dve.wait_ge(*mid_u_ready.at(body, 1))
                for t in range(NT):
                    ins = V_.tensor_tensor_reduce(square[:, t, :], u[:, t, 0:D], u[:, t, 0:D], 1.0, 0.0,
                                                  ALU.mult, ALU.add, powin[:, t:t + 1])
                ins.then_inc(mid_pow_in.sem, 1)
                dve.wait_ge(*mid_pow_out.at(body, 2))
                then(body, V_.tensor_scalar(rnorm[:, :], powout[:, 0:4], RECIP_CAP, None, ALU.min))
                V_.tensor_copy(rnorm_w[:, :, :], rnorm[:, :].unsqueeze(2).to_broadcast([P, NT, P]))\
                    .then_inc(rnorm_ready.sem, 1)

            def norm_products(body):
                dve.wait_ge(*read_out(body, "RROW"))
                for t in range(NT):
                    ins = V_.tensor_scalar(sim[:, t, :], rrow[:, :], rnorm[:, t:t + 1], 1.0 / COS_EPS, ALU.mult, ALU.min)
                then(body, ins)

            def similarity(body, t):
                i = bank_of(body, f"DOTS{t}")
                dve.wait_ge(*filled(body, f"DOTS{t}"))
                V_.tensor_tensor(sim[:, t, :], sim[:, t, :], W[i][:, :], ALU.mult).then_inc(w_free[i].sem, 1)

            def attended(body, a):
                i = bank_of(body, f"AV{a}")
                dve.wait_ge(*filled(body, f"AV{a}"))
                bank = W[i][:, 0:2 * (D + 1)].rearrange("p (i c) -> p i c", i=2)
                then(body, V_.reciprocal(recip_m[:, 2 * a:2 * a + 2], bank[:, :, D]))
                for k in range(2):
                    t = 2 * a + k
                    ins = V_.scalar_tensor_tensor(out=n[:, t, :], in0=bank[:, k, 0:D], scalar=recip_m[:, t:t + 1],
                                                  in1=u[:, t, 0:D], op0=ALU.mult, op1=ALU.add)
                ins.then_inc(w_free[i].sem, 1)
                if a == 1:
                    dve.wait_ge(*read_out(body, "AV0"))
                    dve.wait_ge(*read_out(body, "AV1"))
                    V_.tensor_tensor(x[:, :, :], x[:, :, :], n[:, :, :], ALU.add).then_inc(x_new.sem, 1)

            def run(body):
                counted.pop(body.kind, None)
                for what, k in EVENTS[body.kind]:
                    if what == "save":
                        save(body)
                    elif what == "mid":
                        mid(body)
                    elif what == "front":
                        front(body)
                    elif what == "max":
                        row_max(body, k)
                    elif what == "nmax":
                        split_max(body)
                    elif what == "sum":
                        out_copy(body, k)
                    elif what == "norm2":
                        norm2(body)
                    elif what == "finish":
                        finish(body)
                    elif what != "work":
                        continue
                    elif k == "RROW":
                        norm_products(body)
                    elif k.startswith("DOTS"):
                        similarity(body, int(k[4:]))
                    elif k.startswith("AV"):
                        attended(body, int(k[2:]))
                    elif k == "LATENT":
                        latent(body)
                    elif k in ("Q", "QR", "K", "KR"):
                        rope(body, k)
                    elif k.startswith("T_OUT"):
                        divide(body, int(k[5:]))
                    elif k == "WO":
                        residual(body)
                    elif k == "LOGIT":
                        choose(body)
                    elif k.startswith("MASK"):
                        mask(body, int(k[4:]))
                assert counted.get(body.kind, 0) == DVE_STEPS[body.kind], counted

            bodies(dve, run)

def rope_tables():
    half = HD // 2
    inv_freq = (np.float32(1.0) / np.power(np.float32(10000.0), np.arange(half, dtype=np.float32) / np.float32(half)))
    angle = np.arange(T, dtype=np.float32)[None, :] * inv_freq.astype(np.float32)[:, None]
    rows = np.tile(np.repeat(angle.astype(np.float64), NH, axis=0), (2, 1))
    return np.cos(rows).astype(np.float32), np.sin(rows).astype(np.float32)


def kernel(**inputs):
    import numpy as _np
    import concourse.bacc as _bacc
    from concourse import mybir as _mybir
    from concourse.bass_utils import run_bass_kernel_spmd as _run

    g = {k: _np.asarray(a) for k, a in inputs.items()}
    f = lambda name: g["L0_ffn_" + name]
    by_dim = lambda m: m.reshape(m.shape[0], NPAIR, 2, HD).transpose(0, 3, 2, 1).reshape(m.shape)
    cos, sin = rope_tables()
    arrays = {
        "x": g["L0_attn_x"],
        "WqT": by_dim(f("Wq").T), "WdkvT": f("Wdkv").T, "WukT": by_dim(f("Wuk").T), "WuvT": f("Wuv").T, "WoT": f("Wo").T,
        "gateT": f("gate_w").T, "gate_b": f("gate_b").reshape(1, NE),
        "b1T": f("b1").reshape(NCH, P).T, "b2": f("b2"),
        "n1": f("norm1_w").reshape(P, 1), "n2": f("norm2_w").reshape(P, 1),
        "ln_g": f("ln_g").reshape(LAT, 1), "ln_b": f("ln_b").reshape(LAT, 1),
        "W1T": f("W1").reshape(NE * HID, D).T,
        "W2T": f("W2").transpose(0, 2, 1).reshape(NCH, P, D).transpose(1, 0, 2),
        "pad_q": _np.zeros((64 // HD - N_SLOT, P, T), _mybir.dt.np(BF16)),
        "pad_k": _np.repeat((_np.arange(64 - MAXROW) < 3).astype(_mybir.dt.np(BF16)), NH * T)
                    .reshape(64 // HD - N_SLOT, P, T),
        "cos": cos, "sin": sin,
    }
    nc = _bacc.Bacc("TRN2", target_bir_lowering=False, num_devices=1)
    arrays = {f"in_{k}": _np.ascontiguousarray(a) for k, a in arrays.items()}
    args = {k[3:]: nc.dram_tensor(k, a.shape, _mybir.dt.from_np(a.dtype), kind="ExternalInput").ap()
            for k, a in arrays.items()}
    out = nc.dram_tensor("out_0", (B, T, D), F32, kind="ExternalOutput").ap()
    program(nc, args.pop("x"), out, args)
    r = _run(nc, [arrays], core_ids=[0])
    return r.results[0]["out_0"]
```

```python
from contextlib import ExitStack

import numpy as np

import concourse.bass as bass
from concourse import mybir

F32 = mybir.dt.float32
BF16 = mybir.dt.bfloat16
F32R = mybir.dt.float32r
I32 = mybir.dt.int32
ALU = mybir.AluOpType
ACT = mybir.ActivationFunctionType
AX = mybir.AxisListType

P = 128
B, T, D = 4, 512, 128
NT = T // P
NH, HD = 16, 8
NPAIR = NH // 2
NG = NH // 4
LAT = 64
NE, HID = 4, 512
NC = HID // P
NCH = NE * NC
NHALF = NPAIR // 2
SLOTS = ((0, 3, 0), (3, 2, 1), (5, 1, 2))
N_SLOT = sum(n for _, n, _ in SLOTS)
MAXROW = HD * N_SLOT
PCOLS = 1280
KT_AT = {0: (0, 0), 1: (512, 128), 3: (896, 384), 2: (1024, 256)}
MASKED = -1e30
HIGH_BITS = -(1 << 12)
SCALE = float(1.0 / np.sqrt(HD))
LN_EPS, RMS_EPS, COS_EPS = 1e-5, 1e-6, 1e-8
RECIP_CAP = 1e18


class Body:

    def __init__(self, kind, b=0):
        self.kind, self.b = kind, b

    def item(self, part):
        return {"front": {"START": 0, "BODY": self.b + 1, "BODY_MID": self.b + B},
                "back": {"BODY": self.b, "BODY_MID": self.b + B - 1, "END": 2 * B - 1},
                "mid": {"BODY_MID": self.b}}[part][self.kind]


class Signal:

    def __init__(self, sem, per):
        self.sem, self.per = sem, per

    def at(self, body, n):
        if isinstance(self.per, dict):
            per = self.per
            before = {"START": 0, "BODY": per["START"], "BODY_MID": per["START"] + (B - 1) * per["BODY"],
                      "END": per["START"] + (B - 1) * per["BODY"] + B * per["BODY_MID"]}[body.kind]
            each = 0 if body.kind in ("START", "END") else per[body.kind]
            return self.sem, body.b * each + (before + n + 1)
        part, each = self.per
        return self.sem, body.item(part) * each + (n + 1)

    def at_end_of(self, item):
        return self.sem, item * self.per[1] + (self.per[1] + 1)


BESIDE_SCORES = {
    "BODY": {4: ["T_N"], 5: ["LATENT"], 7: ["Q", ("sum", 0)], 8: ["T_Z", "QR"], 10: ["T_OUT0"], 11: ["K"], 12: ["KR"],
             13: [("sum", 1)], 16: ["T_OUT1"], 19: [("sum", 2)], 22: ["T_OUT2"]},
    "BODY_MID": {4: ["T_U"], 5: ["RROW", "DOTS0", "DOTS1"], 7: ["DOTS2", "DOTS3", ("sum", 0)],
             9: ["AV0", "AV1", "T_OUT0"], 11: [("front", 0)], 13: [("sum", 1)], 14: ["T_N", "LATENT"], 16: ["Q"],
             17: ["T_Z"], 18: ["QR"], 19: ["K"], 20: ["KR", "T_OUT1"], 22: [("sum", 2)], 23: ["T_OUT2"]},
    "END": {7: [("sum", 0)], 13: ["T_OUT0"], 14: [("sum", 1)], 17: ["T_OUT1"], 19: [("sum", 2)], 23: ["T_OUT2"]},
}
BESIDE_STEPS = {"BODY": {"T_O": 1, "WO": 1, "T_N2": 2, "LOGIT": 1, "MASK0": 2},
                "BODY_MID": {"T_O": 0, "WO": 0, "T_N2": 5, "LOGIT": 4, "MASK0": 2}}
BESIDE_CHUNKS = {"BODY": (2, 2), "BODY_MID": (2, 2)}
N_SCORE, N_MAX = 3 * NPAIR, NPAIR * NT


def events(kind):
    out = []

    def add(*names):
        out.extend(("work", x) if isinstance(x, str) else x for x in names)

    if kind == "START":
        add(("front", 0), ("setup", 0), "T_N", "LATENT", "Q", "QR", "T_Z", "K", "KR", "V", ("setup", 1))
        add(*(("max", m) for m in range(N_MAX)), ("nmax", 0), "T_NMAX")
        return out
    add(({"BODY": "front", "BODY_MID": "mid", "END": "save"}[kind], 0))
    for unit in range(N_SCORE):
        add(("score", unit))
        for x in BESIDE_SCORES[kind].get(unit, ()):
            add(x)
    add(("sum", NG - 1))
    nxt = kind != "END"
    if nxt:
        add("V")
    add("T_OUT3")
    steps, chunks = BESIDE_STEPS.get(kind), BESIDE_CHUNKS.get(kind)
    m = 0

    def maxima(k):
        nonlocal m
        for _ in range(k if nxt else 0):
            if m < N_MAX:
                add(("max", m))
                m += 1
                if m == N_MAX:
                    add(("nmax", 0))
    for x in ("T_O", "WO", "T_N2", "LOGIT", "MASK0"):
        if x == "T_N2":
            add(("norm2", 0))
        add(x)
        maxima(nxt and steps[x])
    add("MASK1")
    turned, full = not nxt, False
    for c in range(NCH):
        add(f"HIDDEN{c}")
        if c == 2:
            add("T_OH")
        if c % NC == 1 and c // NC + 2 < NE:
            add(f"MASK{c // NC + 2}")
        if c:
            add(("second", c - 1))
        if full and not turned:
            add("T_NMAX")
            turned = True
        full = m == N_MAX
        maxima(nxt and chunks[c % len(chunks)])
    assert m == N_MAX or not nxt
    add(("second", NCH - 1), ("finish", 0))
    return out


EVENTS = {kind: events(kind) for kind in ("START", "BODY", "BODY_MID", "END")}
for chain in (["T_U", "RROW", *(f"DOTS{t}" for t in range(NT)), "AV0", "AV1", "front", "T_N", "LATENT", "T_Z", "K", "KR",
               "V"], ["T_N", "Q", "QR", "V"], [f"T_OUT{g}" for g in range(NG)]):
    for ev in EVENTS.values():
        names = [k if what == "work" else what for what, k in ev]
        at = [names.index(x) for x in chain if x in names]
        assert at == sorted(at)
WORK = {kind: [x for what, x in ev if what == "work"] for kind, ev in EVENTS.items()}
SCORES = {kind: [e for e in ev if e[0] in ("score", "max")] for kind, ev in EVENTS.items()}


def uses(table, bank):
    return {kind: len(stages[bank::2]) for kind, stages in table.items()}


DVE_STEPS = {"START": 12, "BODY": 23, "BODY_MID": 28, "END": 11}


def program(nc, x_in, out, w):
    ctx = ExitStack()
    with ctx:
        def sb(name, shape, dt=F32):
            return ctx.enter_context(nc.sbuf_tensor(name, shape, dt))

        def sem(name):
            return ctx.enter_context(nc.semaphore(name))

        signals = []

        def signal(name, per):
            signals.append(Signal(sem(name), per))
            return signals[-1]

        between = nc.dram_tensor("between", [B, T, D], F32, kind="Internal").ap()
        q_stack_d = nc.dram_tensor("q_stack_d", [64 // HD, P, T], BF16, kind="Internal").ap()
        k_stack_d = nc.dram_tensor("k_stack_d", [64 // HD, P, T], BF16, kind="Internal").ap()
        nmax_d = nc.dram_tensor("nmax_d", [3 * NH, T], BF16, kind="Internal").ap()

        wq = sb("wq", [P, 2, P])
        wdkv = sb("wdkv", [P, LAT])
        wukv_raw = sb("wukv_raw", [LAT, 2 * P])
        lat_affine = sb("lat_affine", [LAT, P])
        wk = sb("wk", [P, 2, P])
        wv = sb("wv", [P, P])
        wo = sb("wo", [P, P])
        gate = sb("gate", [P, NE])
        gate_b = sb("gate_b", [P, NE])
        w1 = sb("w1", [P, 2, NE * HID])
        w2 = sb("w2", [P, NCH, D])
        b1 = sb("b1", [P, NCH])
        b2 = sb("b2", [NE, D])
        relu_b1 = sb("relu_b1", [P, NCH])
        relu_b1_by_e = sb("relu_b1_by_e", [P, NCH, NE])
        idle_sum = sb("idle_sum", [P, 1])
        own_bias = sb("own_bias", [NE, D])
        n1w = sb("n1w", [P, 1])
        n2w = sb("n2w", [P, 1])
        lng = sb("lng", [LAT, 1])
        lnb = sb("lnb", [LAT, 1])
        cos = sb("cos", [P, T])
        sin = sb("sin", [P, T])
        ident = sb("ident", [P, P])
        ident_b = sb("ident_b", [P, P], BF16)
        mask_q = sb("mask_q", [P, P], BF16)
        mask_k = sb("mask_k", [P, P], BF16)
        rank = sb("rank", [P, NT, NE])
        half_pow = sb("half_pow", [P, 8])

        x = sb("x", [P, NT, D])
        u = sb("u", [P, NT, D + 1])
        n = sb("n", [P, NT, D])
        stats = sb("stats", [P, NT, 6])
        mv = sb("mv", [P, NT, 2])
        u_saved = sb("u_saved", [P, NT, D])
        recip_m = sb("recip_m", [P, NT])
        powin_b = sb("powin_b", [P, NT])
        powout_b = sb("powout_b", [P, NT])
        met = sb("met", [P, 1])
        met_act = sb("met_act", [P, 1])
        zero = sb("zero", [P, 1])
        powin = sb("powin", [P, 8])
        powout = sb("powout", [P, 8])
        nT = sb("nT", [P, T])
        zn = sb("zn", [P, NT, P])
        znT = sb("znT", [P, T])
        rope_a = sb("rope_a", [P, 2, T])
        rope_b = sb("rope_b", [P, 2, T])
        qk = sb("qk", [P, 2, T])
        rest = sb("rest", [P, 2, T])
        parts = sb("parts", [P, 2, 3, T], BF16)
        qs = sb("qs", [P, NPAIR, T], BF16)
        kz = sb("kz", [P, 2, NPAIR, T], BF16)
        v = sb("v", [P, NT, NH, 32])
        nmax = sb("nmax", [P, NT, NH])
        nmax_rest = sb("nmax_rest", [P, NT, NH])
        nmax_parts = sb("nmax_parts", [P, NT, P], BF16)
        nmaxT = sb("nmaxT", [3 * NH, T], BF16)
        pT = sb("pT", [P, 2, 4, PCOLS])
        oT_raw = sb("oT_raw", [P, NG, T])
        recip = sb("recip", [P, NT, 4])
        o = sb("o", [P, NT, D])
        oT = sb("oT", [P, T])
        x2 = sb("x2", [P, NT, D])
        square = sb("square", [P, NT, D])
        n2 = sb("n2", [P, NT, D])
        n2T = sb("n2T", [P, T])
        base = sb("base", [P, NT, D])
        base_next = sb("base_next", [P, NT, D])
        logit = sb("logit", [P, NT, NE])
        top = sb("top", [P, NT])
        onehot = sb("onehot", [P, NT, NE], BF16)
        ohT = sb("ohT", [NE, T])
        n2T_high = sb("n2T_high", [P, T])
        n2T_low = sb("n2T_low", [P, T])
        high_bits = sb("high_bits", [P, 1], I32)
        xe = sb("xe", [P, NE, T])
        xe_low = sb("xe_low", [P, NE, T])
        hid = sb("hid", [P, 4, T])
        yT = sb("yT", [P, T])
        res = sb("res", [P, NT, D])
        rnorm = sb("rnorm", [P, NT])
        rrow = sb("rrow", [P, T])
        sim = [rope_a[:, 0, :], rope_a[:, 1, :], rope_b[:, 0, :], rope_b[:, 1, :]]
        esim = hid

        SC = [ctx.enter_context(nc.psum_tensor(f"score{i}", [P, 2, 512], F32)) for i in range(2)]
        W = [ctx.enter_context(nc.psum_tensor(f"work{i}", [P, 512], F32)) for i in range(2)]
        A = [ctx.enter_context(nc.psum_tensor(f"accum{i}", [P, 512], F32)) for i in range(2)]

        w1_raw, w1_high = [pT[:, i, :, :].rearrange("p h n -> p (h n)")[:, 0:NE * HID] for i in range(2)]

        loads = sem("loads")
        late_loads = sem("late_loads")
        cleared = sem("cleared")
        setup_pe = sem("setup_pe")
        setup_dve = sem("setup_dve")
        setup_pool = sem("setup_pool")
        padded = sem("padded")
        x_loaded = signal("x_loaded", ("front", 16))
        x_read = signal("x_read", ("front", 1))
        pow_in = signal("pow_in", ("front", 2))
        pow_out = signal("pow_out", ("front", 2))
        mid_pow_in = signal("mid_pow_in", ("mid", 2))
        mid_pow_out = signal("mid_pow_out", ("mid", 2))
        back_pow_in = signal("back_pow_in", ("back", 1))
        back_pow_out = signal("back_pow_out", ("back", 1))
        dve_step = signal("dve_step", DVE_STEPS)
        pool_step = signal("pool_step", ("front", 3))
        n_ready = signal("n_ready", ("front", 1))
        mid_u_ready = signal("mid_u_ready", ("mid", 1))
        q_ready = signal("q_ready", ("front", 1))
        parts_ready = [signal(f"parts_ready{s}", ("front", 1)) for s in "qk"]
        stack_stored = [signal(f"{s}_stack_stored", ("front", 16 * len(SLOTS))) for s in "qk"]
        stack_loaded = [signal(f"stack_loaded{i}", ("front", 16 * 4)) for i in range(2)]
        nmax_ready = signal("nmax_ready", ("front", 1))
        nmax_stored = signal("nmax_stored", ("front", 16))
        nmax_loaded = signal("nmax_loaded", ("front", 32))
        sc_full = [signal(f"sc_full{i}", uses(SCORES, i)) for i in range(2)]
        sc_free = [signal(f"sc_free{i}", uses(SCORES, i)) for i in range(2)]
        w_full = [signal(f"w_full{i}", uses(WORK, i)) for i in range(2)]
        w_free = [signal(f"w_free{i}", uses(WORK, i)) for i in range(2)]
        a_full = [signal(f"a_full{i}", ("back", 3 - i)) for i in range(2)]
        a_free = [signal(f"a_free{i}", ("back", 2)) for i in range(2)]
        n2_ready = signal("n2_ready", ("back", 1))
        onehot_ready = signal("onehot_ready", ("back", 1))
        n2T_split = signal("n2T_split", ("back", 1))
        y_step = signal("y_step", ("back", NCH))
        yT_ready = signal("yT_ready", ("back", 1))
        res_ready = signal("res_ready", ("back", 1))
        out_stored = signal("out_stored", ("back", 16))
        rnorm_ready = signal("rnorm_ready", ("mid", 1))
        exp_ready = signal("exp_ready", ("mid", NT))
        x_new = signal("x_new", ("mid", 1))
        setup_steps = sem("setup_steps")

        block = ctx.enter_context(nc.Block())

        def work(body, name):
            k = WORK[body.kind].index(name)
            return k % 2, k // 2 + 1

        def filled(body, name):
            i, k = work(body, name)
            return w_full[i].at(body, k)

        def read_out(body, name):
            i, k = work(body, name)
            return w_free[i].at(body, k)

        def bank_of(body, name):
            return work(body, name)[0]

        def scores(body, what, unit):
            k = SCORES[body.kind].index((what, unit))
            return k % 2, k // 2 + 1

        def bodies(eng, run):
            run(Body("START"))
            with eng.Fori(0, B - 1) as b:
                run(Body("BODY", b))
            with eng.Fori(0, B) as b:
                run(Body("BODY_MID", b))
            run(Body("END"))

        @block.sync
        def _(sp):
            for s in signals:
                sp.sem_inc(s.sem, 1)
            sp.dma_start(x[:, :, :], x_in[0].rearrange("(t p) d -> p t d", p=P)).then_inc(x_loaded.sem, 16)
            for dst, src in ((n1w[:, :], w["n1"]), (lng[:, :], w["ln_g"]), (lnb[:, :], w["ln_b"]),
                             (wdkv[:, :], w["WdkvT"]), (wukv_raw[:, 0:P], w["WukT"]), (wukv_raw[:, P:], w["WuvT"]),
                             (wq[:, 0, :], w["WqT"]), (cos[:, :], w["cos"]), (sin[:, :], w["sin"])):
                sp.dma_start(dst, src).then_inc(loads, 16)
            for dst, src in ((b1[:, :], w["b1T"]), (w2[:, :, :], w["W2T"]), (w1_raw, w["W1T"]), (n2w[:, :], w["n2"]),
                             (gate[:, :], w["gateT"]), (gate_b[:, :], w["gate_b"].to_broadcast([P, NE])),
                             (b2[:, :], w["b2"]), (wo[:, :], w["WoT"])):
                sp.dma_start(dst, src).then_inc(late_loads, 16)
            for stack, pad in ((q_stack_d, "pad_q"), (k_stack_d, "pad_k")):
                sp.dma_start(stack[N_SLOT:, :, :], w[pad]).then_inc(padded, 16)

            def load_x(src):
                sp.dma_start(x[:, :, :], src.rearrange("(t p) d -> p t d", p=P)).then_inc(x_loaded.sem, 16)

            def store_stacks(body):
                for s, stack in enumerate((q_stack_d, k_stack_d)):
                    sp.wait_ge(*parts_ready[s].at(body, 1))
                    for first, n, part in SLOTS:
                        src = parts[:, 1, 0:n, :] if s else parts[:, 0, part:part + 1, :].to_broadcast([P, n, T])
                        sp.dma_start(stack[first:first + n].rearrange("s m n -> m s n"), src)\
                          .then_inc(stack_stored[s].sem, 16)
                    if s == 0:
                        load_q(body, 0)

            def rows_of(stack, j, half):
                return stack.rearrange("s (d j p) n -> j (s d) p n", d=HD, j=2)[j, :, NHALF * half:NHALF * (half + 1)]

            def load_q(body, half):
                if body.kind != "START":
                    for i in range(2):
                        unit = [u for u in range(N_SCORE * (half + 1) // 2) if scores(body, "score", u)[0] == i][-1]
                        sp.wait_ge(*sc_full[i].at(body, scores(body, "score", unit)[1]))
                if half == 0:
                    sp.wait_ge(*stack_stored[0].at(body, stack_stored[0].per[1]))
                for j in range(2):
                    sp.dma_start(qs[64 * j:64 * j + 64, NHALF * half:NHALF * (half + 1), :], rows_of(q_stack_d, j, half))\
                      .then_inc(stack_loaded[half].sem, 16)

            def load_k(half):
                for j in range(2):
                    sp.dma_start(kz[64 * j:64 * j + 64, j, NHALF * half:NHALF * (half + 1), :],
                                 rows_of(k_stack_d, j, half)).then_inc(stack_loaded[half].sem, 16)

            def load_nmax(body):
                sp.wait_ge(*read_out(body, "T_NMAX"))
                sp.dma_start(nmax_d, nmaxT[:, :]).then_inc(nmax_stored.sem, 16)
                sp.wait_ge(*nmax_stored.at(body, 16))
                for j in range(2):
                    r = 64 * j + MAXROW
                    sp.dma_start(qs[r:r + 3, :, :], nmax_d.rearrange("(s p j) n -> j s p n", s=3, j=2)[j])\
                      .then_inc(nmax_loaded.sem, 16)

            def store_result(body, dst):
                sp.wait_ge(*res_ready.at(body, 1))
                sp.dma_start(dst.rearrange("(t p) d -> p t d", p=P), res[:, :, :]).then_inc(out_stored.sem, 16)

            def front(body, x_next):
                if x_next is not None:
                    sp.wait_ge(*x_read.at(body, 1))
                    load_x(x_next)
                store_stacks(body)
                sp.wait_ge(*stack_stored[1].at(body, stack_stored[1].per[1]))
                load_k(0)
                load_q(body, 1)
                load_k(1)
                load_nmax(body)

            def beside(body, dst, x_next):
                front(body, x_next)
                store_result(body, dst)

            sp.wait_ge(cleared, 1)
            sp.wait_ge(padded, 32)
            front(Body("START"), x_in[1])
            with sp.Fori(0, B - 2) as b:
                beside(Body("BODY", b), between[b], x_in[b + 2])
            sp.wait_ge(out_stored.sem, 16 * (B - 2) + 1)
            beside(Body("BODY", B - 2), between[B - 2], between[0])
            beside(Body("BODY_MID", 0), between[B - 1], between[1])
            sp.wait_ge(out_stored.sem, 16 * B + 1)
            with sp.Fori(1, B - 1) as b:
                beside(Body("BODY_MID", b), out[b - 1], between[b + 1])
            beside(Body("BODY_MID", B - 1), out[B - 2], None)
            store_result(Body("END"), out[B - 1])
            sp.wait_ge(out_stored.sem, 2 * 16 * B + 1)

        @block.gpsimd
        def _(pool):
            pool.memset(zero[:, :], 0.0)
            pool.memset(nmax_parts[:, :, :], 0.0)
            pool.memset(half_pow[:, :], -0.5)
            pool.memset(ident[:, :], 0.0)
            pool.memset(ident_b[:, :], 0.0)
            pool.memset(mask_q[:, :], 0.0)
            pool.memset(mask_k[:, :], 0.0)
            pool.memset(lat_affine[:, :], 0.0)
            pool.memset(zn[:, :, :], 0.0)
            pool.memset(v[:, :, :, :], 0.0)
            for e in range(NE):
                pool.memset(rank[:, :, e:e + 1], float(NE - e))
            pool.memset(relu_b1_by_e[:, :, :], 0.0)
            pool.memset(u[:, :, D:D + 1], 1.0).then_inc(setup_pool, 1)
            pool.wait_ge(setup_pool, 1)
            pool.memset(zn[:, :, LAT:LAT + 1], 1.0)
            pool.memset(v[:, :, :, HD:HD + 1], 1.0)
            for m in (ident, ident_b):
                pool.affine_select(out=m[:, :], in_=m[:, :], compare_op=ALU.not_equal, fill=1.0, base=0,
                                   pattern=[[-1, P]], channel_multiplier=1)
            pool.affine_select(out=mask_q[:, :], in_=mask_q[:, :], compare_op=ALU.is_ge, fill=MASKED, base=0,
                               pattern=[[-1, P]], channel_multiplier=1)
            pool.affine_select(out=mask_k[:, :], in_=mask_k[:, :], compare_op=ALU.is_ge, fill=MASKED, base=0,
                               pattern=[[1, P]], channel_multiplier=-1).then_inc(setup_pool, 1)

            def power(body, asked, given, k, dst, src, cols):
                pool.wait_ge(*asked.at(body, k))
                pool.tensor_tensor(dst[:, 0:cols], src[:, 0:cols], half_pow[:, 0:cols], ALU.pow).then_inc(given.sem, 1)

            def split_q(body):
                zeros = zero[:, 0:1].to_broadcast([P, T])
                pool.wait_ge(*stack_stored[0].at(body, 0))
                pool.wait_ge(*q_ready.at(body, 1))
                pool.tensor_tensor(parts[:, 0, 0, :], qk[:, 0, :], zeros, ALU.add).then_inc(pool_step.sem, 1)
                pool.wait_ge(*pool_step.at(body, 1))
                pool.tensor_tensor(rest[:, 0, :], qk[:, 0, :], parts[:, 0, 0, :], ALU.subtract).then_inc(pool_step.sem, 1)
                pool.wait_ge(*pool_step.at(body, 2))
                pool.tensor_tensor(parts[:, 0, 1, :], rest[:, 0, :], zeros, ALU.add).then_inc(pool_step.sem, 1)
                pool.wait_ge(*pool_step.at(body, 3))
                pool.tensor_tensor(parts[:, 0, 2, :], rest[:, 0, :], parts[:, 0, 1, :], ALU.subtract)\
                    .then_inc(parts_ready[0].sem, 1)

            def run(body):
                if body.kind == "BODY_MID":
                    power(body, mid_pow_in, mid_pow_out, 1, powout, powin, 4)
                    power(body, mid_pow_in, mid_pow_out, 2, powout, powin, 4)
                if body.kind != "END":
                    power(body, pow_in, pow_out, 1, powout, powin, 8)
                    power(body, pow_in, pow_out, 2, powout, powin, 4)
                    split_q(body)
                if body.kind != "START":
                    power(body, back_pow_in, back_pow_out, 1, powout_b, powin_b, 4)

            bodies(pool, run)

        @block.scalar
        def _(act):
            def copy(body, name, dst, src):
                i = bank_of(body, name)
                act.wait_ge(*filled(body, name))
                nc.scalar.activation(dst, src(W[i]), ACT.Copy).then_inc(w_free[i].sem, 1)

            def whole(bank):
                return bank[:, :]

            def exponential(body, unit):
                p, z = unit // 3, unit % 3
                g, half = p // 2, 2 * (p % 2)
                if unit % 6 == 0:
                    act.wait_ge(*a_full[g % 2].at(body, g // 2))
                i, k = scores(body, "score", unit)
                act.wait_ge(*sc_full[i].at(body, k))
                if z < 2:
                    ins = nc.scalar.activation(pT[:, g % 2, half + z, 0:1024],
                                               SC[i][:, :, :].rearrange("p a n -> p (a n)"), ACT.Exp, scale=SCALE)
                else:
                    ins = nc.scalar.activation(pT[:, g % 2, half:half + 2, 1024:PCOLS],
                                               SC[i][:, 0, :].rearrange("p (j n) -> p j n", j=2),
                                               ACT.Exp, scale=SCALE)
                ins.then_inc(sc_free[i].sem, 1)

            def run(body):
                for what, k in EVENTS[body.kind]:
                    if what == "score":
                        exponential(body, k)
                    elif what != "work":
                        continue
                    elif k == "T_U":
                        copy(body, k, nT[:, :], whole)
                    elif k == "RROW":
                        copy(body, k, rrow[:, :], whole)
                    elif k.startswith("DOTS"):
                        t = int(k[4:])
                        act.wait_ge(*read_out(body, k))
                        nc.scalar.activation(esim[:, t, :], sim[t], ACT.Exp).then_inc(exp_ready.sem, 1)
                    elif k == "T_N":
                        copy(body, k, nT[:, :], whole)
                    elif k == "T_Z":
                        copy(body, k, znT[:, :], whole)
                    elif k == "V":
                        if body.kind == "START":
                            act.wait_ge(late_loads, 16 * 8)
                            act.wait_ge(setup_pool, 2)
                        else:
                            act.wait_ge(*a_full[1].at(body, 2))
                        copy(body, k, v[:, :, :, 0:HD],
                             lambda bank: bank[:, :].rearrange("p (t h d) -> p t h d", t=NT, d=HD))
                    elif k == "T_NMAX":
                        copy(body, k, nmaxT[:, :], lambda bank: bank[0:3 * NH, :].bitcast(BF16)[:, 0:T])
                    elif k == "T_O":
                        copy(body, k, oT[:, :], whole)
                    elif k == "T_N2":
                        copy(body, k, n2T[:, :], whole)
                    elif k == "T_OH":
                        copy(body, k, ohT[:, :], lambda bank: bank[0:NE, :].bitcast(BF16)[:, 0:T])
                    elif k.startswith("HIDDEN"):
                        c = int(k[6:])
                        i = bank_of(body, k)
                        act.wait_ge(*filled(body, k))
                        if c >= 4:
                            act.wait_ge(*y_step.at(body, c - 3))
                        nc.scalar.activation(hid[:, c % 4, :], W[i][:, :], ACT.Relu, bias=b1[:, c:c + 1])\
                            .then_inc(w_free[i].sem, 1)

            act.wait_ge(setup_pool, 1)
            nc.scalar.activation(met_act[:, :], zero[:, :], ACT.Exp)
            bodies(act, run)

        @block.tensor
        def _(pe):
            def setup_latent():
                pe.wait_ge(setup_dve, 1)
                pe.matmul(A[1][:, 0:2 * P], lat_affine[:, :], wukv_raw[:, :], start=True, stop=True)\
                  .then_inc(setup_pe, 1)

            def setup_experts():
                pe.wait_ge(setup_dve, 3)
                for c in range(NCH):
                    pe.matmul(A[1][:, 0:1], w2[:, c, :], relu_b1[:, c:c + 1], start=(c == 0), stop=(c == NCH - 1))
                for c in range(NCH):
                    last = pe.matmul(A[0][0:NE, 0:D], relu_b1_by_e[:, c, :], w2[:, c, :],
                                     start=(c == 0), stop=(c == NCH - 1))
                last.then_inc(setup_pe, 1)

            def transposes(src, rows=P):
                def emit(bank):
                    for t in range(NT):
                        last = pe.transpose(bank[0:rows, t * P:(t + 1) * P], src(t), ident[:, :])
                    return last
                return emit

            def product(lhsT, rhs):
                return lambda bank: pe.matmul(bank[:, :], lhsT, rhs, start=True, stop=True)

            def hidden(c):
                high, low = [w1[:, i, c * P:(c + 1) * P].bitcast(F32R) for i in range(2)]
                x_high, x_low = [part[:, c // NC, :].bitcast(F32R) for part in (xe, xe_low)]

                def emit(bank):
                    pe.matmul(bank[:, :], high, x_high, start=True, stop=False)
                    pe.matmul(bank[:, :], high, x_low, start=False, stop=False)
                    return pe.matmul(bank[:, :], low, x_high, start=False, stop=True)
                return emit

            def by_token(src, weight, cols):
                def emit(bank):
                    for t in range(NT):
                        last = pe.matmul(bank[:, t * cols:(t + 1) * cols], src[:, t * P:(t + 1) * P], weight,
                                         start=True, stop=True)
                    return last
                return emit

            def turn_max(bank):
                for t in range(NT):
                    last = pe.transpose(bank[:, :].bitcast(BF16)[:, t * P:(t + 1) * P], nmax_parts[:, t, :],
                                        ident_b[:, :])
                return last

            def turn_onehot(bank):
                for t in range(NT):
                    last = pe.transpose(bank[0:NE, :].bitcast(BF16)[:, t * P:(t + 1) * P], onehot[:, t, :],
                                        ident_b[:, :])
                return last

            def spread(e):
                def emit(bank):
                    for t in range(NT):
                        last = pe.matmul(bank[:, t * P:(t + 1) * P], onehot[:, t, e:e + 1].to_broadcast([P, P]),
                                         ident_b[:, :], start=True, stop=True)
                    return last
                return emit

            def norm_rows(bank):
                for t in range(NT):
                    last = pe.matmul(bank[:, t * P:(t + 1) * P], rnorm[:, t:t + 1].to_broadcast([P, P]), ident[:, :],
                                     start=True, stop=True)
                return last

            def attend(a):
                def emit(bank):
                    for i in range(2):
                        q0 = (2 * a + i) * P
                        for t in range(NT):
                            last = pe.matmul(bank[:, i * (D + 1):(i + 1) * (D + 1)], esim[:, t, q0:q0 + P], u[:, t, :],
                                             start=(t == 0), stop=(t == NT - 1))
                    return last
                return emit

            def stage(body, name):
                if name == "T_U":
                    pe.wait_ge(*mid_u_ready.at(body, 1))
                    return transposes(lambda t: u[:, t, 0:D])
                if name == "RROW":
                    pe.wait_ge(*rnorm_ready.at(body, 1))
                    return norm_rows
                if name.startswith("DOTS"):
                    t = int(name[4:])
                    if t == 0:
                        pe.wait_ge(*read_out(body, "T_U"))
                    return product(nT[:, t * P:(t + 1) * P], nT[:, :])
                if name.startswith("AV"):
                    pe.wait_ge(*exp_ready.at(body, NT))
                    return attend(int(name[2:]))
                if name == "T_N":
                    pe.wait_ge(*n_ready.at(body, 1))
                    return transposes(lambda t: n[:, t, :])
                if name == "LATENT":
                    pe.wait_ge(*read_out(body, "T_N"))
                    return by_token(nT, wdkv[:, :], LAT)
                if name in ("Q", "QR"):
                    return product(wq[:, ("Q", "QR").index(name), :], nT[:, :])
                if name == "T_Z":
                    pe.wait_ge(*read_out(body, "LATENT"))
                    return transposes(lambda t: zn[:, t, :])
                if name in ("K", "KR"):
                    if body.kind == "START":
                        pe.wait_ge(setup_dve, 2)
                    pe.wait_ge(*read_out(body, "T_Z"))
                    return product(wk[:, ("K", "KR").index(name), :], znT[:, :])
                if name == "V":
                    return by_token(znT, wv[:, :], P)
                if name == "T_NMAX":
                    pe.wait_ge(*nmax_ready.at(body, 1))
                    return turn_max
                if name.startswith("T_OUT"):
                    g = int(name[5:])
                    pe.wait_ge(*a_free[g % 2].at(body, g // 2 + 1))
                    return transposes(lambda t: oT_raw[:, g, t * P:(t + 1) * P])
                if name == "T_O":
                    pe.wait_ge(*read_out(body, f"T_OUT{NG - 1}"))
                    return transposes(lambda t: o[:, t, :])
                if name == "WO":
                    pe.wait_ge(*read_out(body, "T_O"))
                    return by_token(oT, wo[:, :], D)
                if name == "T_N2":
                    pe.wait_ge(*n2_ready.at(body, 1))
                    return transposes(lambda t: n2[:, t, :])
                if name == "LOGIT":
                    pe.wait_ge(*read_out(body, "T_N2"))
                    return by_token(n2T, gate[:, :], NE)
                if name == "T_OH":
                    return turn_onehot
                if name.startswith("MASK"):
                    if name == "MASK0":
                        pe.wait_ge(*onehot_ready.at(body, 1))
                    return spread(int(name[4:]))
                c = int(name[6:])
                pe.wait_ge(*read_out(body, f"MASK{c // NC}"))
                return hidden(c)

            def max_unit(body, unit):
                p, qt = unit // NT, unit % NT
                cols = (qt + 1) * P
                if unit in (0, N_MAX // 2):
                    half = unit // (N_MAX // 2)
                    pe.wait_ge(*stack_loaded[half].at(body, stack_loaded[half].per[1]))
                i, k = scores(body, "max", unit)
                pe.wait_ge(*sc_free[i].at(body, k - 1))
                for j in range(2):
                    pe.matmul(SC[i][:, j, 0:cols], qs[:, p, qt * P:(qt + 1) * P], kz[:, j, p, 0:cols],
                              start=True, stop=False)
                    last = pe.matmul(SC[i][:, j, cols - P:cols], ident_b[:, :], mask_q[:, :], start=False, stop=True)
                last.then_inc(sc_full[i].sem, 1)

            def key_tile(bank, at, p, h, kt):
                q0 = kt * P
                pe.matmul(bank[:, at:at + T - q0], kz[:, h % 2, p, q0:q0 + P], qs[:, p, q0:T], start=True, stop=False)
                return pe.matmul(bank[:, at:at + P], ident_b[:, :], mask_k[:, :], start=False, stop=True)

            def score_unit(body, unit):
                p, z = unit // 3, unit % 3
                i, k = scores(body, "score", unit)
                pe.wait_ge(*sc_free[i].at(body, k - 1))
                if z < 2:
                    h = 2 * p + z
                    key_tile(SC[i][:, 0], 0, p, h, 0)
                    key_tile(SC[i][:, 1], 0, p, h, 1)
                    last = key_tile(SC[i][:, 1], 384, p, h, 3)
                else:
                    key_tile(SC[i][:, 0], 0, p, 2 * p, 2)
                    last = key_tile(SC[i][:, 0], 256, p, 2 * p + 1, 2)
                last.then_inc(sc_full[i].sem, 1)

            def weighted_sum(body, g):
                a = g % 2
                for i in range(2):
                    unit = [q for q in range(6 * g, 6 * g + 6) if scores(body, "score", q)[0] == i][-1]
                    pe.wait_ge(*sc_free[i].at(body, scores(body, "score", unit)[1]))
                if g < 2:
                    pe.wait_ge(*(res_ready, yT_ready)[g].at(body, 0))
                else:
                    pe.wait_ge(*a_free[a].at(body, 1))
                for i, (kt, (at, q0)) in enumerate(KT_AT.items()):
                    for j in range(4):
                        last = pe.matmul(A[a][32 * j:32 * j + 32, q0:T], v[:, kt, 4 * g + j, :],
                                         pT[:, a, j, at:at + T - q0], start=(i == 0), stop=(i == NT - 1))
                last.then_inc(a_full[a].sem, 1)

            def second(body, c):
                if c == 0:
                    pe.wait_ge(*a_free[1].at(body, 2))
                if c == NCH // 2:
                    pe.wait_ge(*read_out(body, "T_OH"))
                    pe.matmul(A[1][:, :], own_bias[:, :], ohT[:, :], start=False, stop=False)
                pe.wait_ge(*read_out(body, f"HIDDEN{c}"))
                pe.matmul(A[1][:, :], w2[:, c, :], hid[:, c % 4, :], start=(c == 0), stop=(c == NCH - 1))\
                    .then_inc(y_step.sem, 1)

            def run(body):
                for what, k in EVENTS[body.kind]:
                    if what == "work":
                        emit = stage(body, k)
                        i, uses_so_far = work(body, k)
                        pe.wait_ge(*w_free[i].at(body, uses_so_far - 1))
                        emit(W[i]).then_inc(w_full[i].sem, 1)
                    elif what == "setup":
                        (setup_latent, setup_experts)[k]()
                    elif what == "score":
                        if k == 0:
                            pe.wait_ge(*nmax_loaded.at_end_of(body.item("back")))
                        score_unit(body, k)
                    elif what == "sum":
                        weighted_sum(body, k)
                    elif what == "max":
                        max_unit(body, k)
                    elif what == "second":
                        second(body, k)
                    elif what == "finish":
                        pe.wait_ge(*yT_ready.at(body, 1))
                        pe.wait_ge(*a_free[0].at(body, 2))
                        for t in range(NT):
                            last = pe.transpose(A[0][:, t * P:(t + 1) * P], yT[:, t * P:(t + 1) * P], ident[:, :])
                        last.then_inc(a_full[0].sem, 1)

            bodies(pe, run)

        @block.vector
        def _(dve):
            V_ = nc.vector
            counted = {}

            def then(body, ins):
                ins.then_inc(dve_step.sem, 1)
                counted[body.kind] = counted.get(body.kind, 0) + 1
                dve.wait_ge(*dve_step.at(body, counted[body.kind]))

            def setup_latent():
                dve.wait_ge(loads, 16 * 9)
                dve.wait_ge(setup_pool, 2)
                V_.tensor_scalar(lat_affine[:, 0:LAT], ident[0:LAT, 0:LAT], lng[:, 0:1], None, ALU.mult)
                V_.tensor_copy(lat_affine[:, LAT:LAT + 1], lnb[:, :])
                V_.tensor_scalar(wdkv[:, :], wdkv[:, :], n1w[:, 0:1], None, ALU.mult)
                V_.tensor_scalar(wq[:, 0, :], wq[:, 0, :], n1w[:, 0:1], None, ALU.mult).then_inc(setup_dve, 1)
                dve.wait_ge(setup_pe, 1)
                V_.tensor_copy(wk[:, 0, :], A[1][:, 0:P])
                V_.tensor_copy(wv[:, :], A[1][:, P:2 * P]).then_inc(setup_steps, 1)
                dve.wait_ge(setup_steps, 1)
                for m in (wq, wk):
                    V_.tensor_scalar(m[:, 1, 0:P // 2], m[:, 0, P // 2:P], -1.0, None, ALU.mult)
                    last = V_.tensor_copy(m[:, 1, P // 2:P], m[:, 0, 0:P // 2])
                last.then_inc(setup_dve, 1)

            def setup_experts():
                dve.wait_ge(late_loads, 16 * 8)
                V_.tensor_scalar(relu_b1[:, :], b1[:, :], 0.0, None, ALU.max).then_inc(setup_steps, 1)
                dve.wait_ge(setup_steps, 2)
                for e in range(NE):
                    last = V_.tensor_copy(relu_b1_by_e[:, e * NC:(e + 1) * NC, e:e + 1],
                                          relu_b1[:, e * NC:(e + 1) * NC].rearrange("p (c o) -> p c o", o=1))
                last.then_inc(setup_dve, 1)
                V_.tensor_scalar(gate[:, :], gate[:, :], n2w[:, 0:1], None, ALU.mult)
                V_.tensor_scalar(w1_raw, w1_raw, n2w[:, 0:1], None, ALU.mult).then_inc(setup_steps, 1)
                dve.wait_ge(setup_steps, 3)
                V_.tensor_tensor(w1_high.bitcast(I32), w1_raw.bitcast(I32), high_bits[:, 0:1].to_broadcast([P, NE * HID]),
                                 ALU.bitwise_and).then_inc(setup_steps, 1)
                dve.wait_ge(setup_steps, 4)
                V_.tensor_copy(w1[:, 0, :].bitcast(F32R), w1_high)
                V_.tensor_tensor(w1[:, 1, :].bitcast(F32R), w1_raw, w1_high, ALU.subtract)
                dve.wait_ge(setup_pe, 2)
                V_.tensor_copy(idle_sum[:, :], A[1][:, 0:1])
                V_.tensor_tensor(own_bias[:, :], A[0][0:NE, 0:D], b2[:, :], ALU.add).then_inc(setup_dve, 1)

            def moments(body, src):
                for t in range(NT):
                    ins = V_.bn_stats(stats[:, t, :], src(t))
                then(body, ins)
                V_.tensor_copy(met[:, :], stats[:, 0, 0:1])
                for t in range(NT):
                    ins = V_.bn_aggr(mv[:, t, :], stats[:, t, :])
                then(body, ins)

            def normed(dst, factor):
                for t in range(NT):
                    ins = V_.tensor_scalar(dst[:, t, 0:D], x[:, t, :], mv[:, t, 0:1], factor[:, t:t + 1],
                                           ALU.subtract, ALU.mult)
                return ins

            def front(body):
                if body.kind == "BODY_MID":
                    dve.wait_ge(*x_new.at(body, 1))
                else:
                    dve.wait_ge(*x_loaded.at(body, 16))
                moments(body, lambda t: x[:, t, :])
                V_.tensor_scalar(powin[:, 4:8], mv[:, :, 1], 1.0 + RMS_EPS, RMS_EPS * LN_EPS, ALU.mult, ALU.add)
                V_.tensor_scalar(powin[:, 0:4], mv[:, :, 1], LN_EPS, None, ALU.add).then_inc(pow_in.sem, 1)
                if body.kind == "BODY":
                    save(body)
                dve.wait_ge(*pow_out.at(body, 1))
                normed(n, powout[:, 4:8]).then_inc(n_ready.sem, 1)
                then(body, normed(u, powout[:, 0:4]))
                V_.scalar_tensor_tensor(out=base_next[:, :, :], in0=u[:, :, 0:D], scalar=0.5, in1=x[:, :, :],
                                        op0=ALU.mult, op1=ALU.add).then_inc(x_read.sem, 1)

            def latent(body):
                i = bank_of(body, "LATENT")
                dve.wait_ge(*filled(body, "LATENT"))
                lat = W[i][:, 0:NT * LAT].rearrange("p (t c) -> p t c", t=NT)
                moments(body, lambda t: lat[:, t, :])
                V_.tensor_scalar(powin[:, 0:4], mv[:, :, 1], LN_EPS, None, ALU.add).then_inc(pow_in.sem, 1)
                dve.wait_ge(*pow_out.at(body, 2))
                for t in range(NT):
                    ins = V_.tensor_scalar(zn[:, t, 0:LAT], lat[:, t, :], mv[:, t, 0:1], powout[:, t:t + 1],
                                           ALU.subtract, ALU.mult)
                ins.then_inc(w_free[i].sem, 1)

            def rope(body, name):
                s = "QK".index(name[0])
                i = bank_of(body, name)
                dve.wait_ge(*filled(body, name))
                if name in "QK":
                    V_.tensor_tensor(rope_a[:, s, :], W[i][:, :], cos[:, :], ALU.mult).then_inc(w_free[i].sem, 1)
                    return
                V_.tensor_tensor(rope_b[:, s, :], W[i][:, :], sin[:, :], ALU.mult).then_inc(w_free[i].sem, 1)
                dve.wait_ge(*read_out(body, name[0]))
                dve.wait_ge(*read_out(body, name))
                if name == "QR":
                    dve.wait_ge(*parts_ready[0].at(body, 0))
                    V_.tensor_tensor(qk[:, s, :], rope_a[:, s, :], rope_b[:, s, :], ALU.add).then_inc(q_ready.sem, 1)
                    return
                then(body, V_.tensor_tensor(qk[:, s, :], rope_a[:, s, :], rope_b[:, s, :], ALU.add))
                dve.wait_ge(*stack_stored[1].at(body, 0))
                then(body, V_.tensor_copy(parts[:, s, 0, :], qk[:, s, :]))
                then(body, V_.tensor_tensor(rest[:, s, :], qk[:, s, :], parts[:, s, 0, :], ALU.subtract))
                then(body, V_.tensor_copy(parts[:, s, 1, :], rest[:, s, :]))
                V_.tensor_tensor(parts[:, s, 2, :], rest[:, s, :], parts[:, s, 1, :], ALU.subtract)\
                  .then_inc(parts_ready[1].sem, 1)

            def row_max(body, unit):
                p, qt = unit // NT, unit % NT
                i, k = scores(body, "max", unit)
                dve.wait_ge(*sc_full[i].at(body, k))
                V_.tensor_reduce(nmax[:, qt, 2 * p:2 * p + 2], SC[i][:, :, 0:(qt + 1) * P], AX.X, ALU.max,
                                 negate=True).then_inc(sc_free[i].sem, 1)

            def split_max(body):
                for i in range(2):
                    unit = [m for m in range(N_MAX) if scores(body, "max", m)[0] == i][-1]
                    dve.wait_ge(*sc_free[i].at(body, scores(body, "max", unit)[1]))
                then(body, V_.tensor_copy(nmax_parts[:, :, 0:NH], nmax[:, :, :]))
                then(body, V_.tensor_tensor(nmax_rest[:, :, :], nmax[:, :, :], nmax_parts[:, :, 0:NH], ALU.subtract))
                then(body, V_.tensor_copy(nmax_parts[:, :, NH:2 * NH], nmax_rest[:, :, :]))
                V_.tensor_tensor(nmax_parts[:, :, 2 * NH:3 * NH], nmax_rest[:, :, :], nmax_parts[:, :, NH:2 * NH],
                                 ALU.subtract).then_inc(nmax_ready.sem, 1)

            def out_copy(body, g):
                dve.wait_ge(*a_full[g % 2].at(body, g // 2 + 1))
                V_.tensor_copy(oT_raw[:, g, :], A[g % 2][:, :]).then_inc(a_free[g % 2].sem, 1)

            def divide(body, g):
                i = bank_of(body, f"T_OUT{g}")
                dve.wait_ge(*filled(body, f"T_OUT{g}"))
                bank = W[i][:, :].rearrange("p (t j c) -> p t j c", t=NT, c=32)
                then(body, V_.reciprocal(recip[:, :, :], bank[:, :, :, HD]))
                V_.tensor_tensor(o[:, :, 4 * HD * g:4 * HD * (g + 1)].rearrange("p t (j d) -> p t j d", d=HD),
                                 bank[:, :, :, 0:HD], recip[:, :, :].unsqueeze(3).to_broadcast([P, NT, 4, HD]),
                                 ALU.mult).then_inc(w_free[i].sem, 1)

            def residual(body):
                i = bank_of(body, "WO")
                dve.wait_ge(*filled(body, "WO"))
                attn = W[i][:, :].rearrange("p (t d) -> p t d", t=NT)
                then(body, V_.tensor_tensor(x2[:, :, :], attn, u_saved[:, :, :], ALU.add))
                for t in range(NT):
                    ins = V_.tensor_tensor_reduce(square[:, t, :], x2[:, t, :], x2[:, t, :], 1.0 / D, RMS_EPS,
                                                  ALU.mult, ALU.add, powin_b[:, t:t + 1])
                ins.then_inc(back_pow_in.sem, 1)
                V_.scalar_tensor_tensor(out=base[:, :, :], in0=attn, scalar=0.5, in1=base[:, :, :],
                                        op0=ALU.mult, op1=ALU.add).then_inc(w_free[i].sem, 1)

            def norm2(body):
                dve.wait_ge(*back_pow_out.at(body, 1))
                for t in range(NT):
                    ins = V_.tensor_scalar(n2[:, t, :], x2[:, t, :], powout_b[:, t:t + 1], None, ALU.mult)
                ins.then_inc(n2_ready.sem, 1)

            def choose(body):
                i = bank_of(body, "LOGIT")
                dve.wait_ge(*filled(body, "LOGIT"))
                V_.tensor_tensor(logit[:, :, :], W[i][:, 0:NT * NE].rearrange("p (t e) -> p t e", t=NT),
                                 gate_b[:, :].unsqueeze(1).to_broadcast([P, NT, NE]), ALU.add)\
                    .then_inc(w_free[i].sem, 1)
                dve.wait_ge(*read_out(body, "LOGIT"))
                for last in (False, True):
                    then(body, V_.tensor_reduce(top[:, :], logit[:, :, :], AX.X, ALU.max))
                    ins = V_.tensor_tensor(onehot[:, :, :], logit[:, :, :],
                                           top[:, :].unsqueeze(2).to_broadcast([P, NT, NE]), ALU.is_equal)
                    if last:
                        ins.then_inc(onehot_ready.sem, 1)
                    else:
                        then(body, ins)
                        then(body, V_.tensor_tensor(logit[:, :, :], onehot[:, :, :], rank[:, :, :], ALU.mult))
                dve.wait_ge(*read_out(body, "T_N2"))
                then(body, V_.tensor_tensor(n2T_high[:, :].bitcast(I32), n2T[:, :].bitcast(I32),
                                            high_bits[:, 0:1].to_broadcast([P, T]), ALU.bitwise_and))
                V_.tensor_tensor(n2T_low[:, :], n2T[:, :], n2T_high[:, :], ALU.subtract).then_inc(n2T_split.sem, 1)

            def mask(body, e):
                i = bank_of(body, f"MASK{e}")
                dve.wait_ge(*filled(body, f"MASK{e}"))
                dve.wait_ge(*n2T_split.at(body, 1))
                V_.tensor_tensor(xe[:, e, :].bitcast(F32R), n2T_high[:, :], W[i][:, :], ALU.mult)
                V_.tensor_tensor(xe_low[:, e, :].bitcast(F32R), n2T_low[:, :], W[i][:, :], ALU.mult)\
                  .then_inc(w_free[i].sem, 1)

            def finish(body):
                dve.wait_ge(*y_step.at(body, NCH))
                V_.tensor_scalar(yT[:, :], A[1][:, :], idle_sum[:, 0:1], None, ALU.subtract).then_inc(yT_ready.sem, 1)
                dve.wait_ge(*a_full[0].at(body, 3))
                dve.wait_ge(*out_stored.at(body, 0))
                V_.scalar_tensor_tensor(out=res[:, :, :], in0=A[0][:, :].rearrange("p (t d) -> p t d", t=NT), scalar=0.5,
                                        in1=base[:, :, :], op0=ALU.mult, op1=ALU.add).then_inc(res_ready.sem, 1)

            def save(body):
                dve.wait_ge(*res_ready.at(body, 0))
                V_.tensor_copy(u_saved[:, :, :], u[:, :, 0:D])
                then(body, V_.tensor_copy(base[:, :, :], base_next[:, :, :]))

            def mid(body):
                dve.wait_ge(*x_loaded.at(body, 16))
                moments(body, lambda t: x[:, t, :])
                V_.tensor_scalar(powin[:, 0:4], mv[:, :, 1], LN_EPS, None, ALU.add).then_inc(mid_pow_in.sem, 1)
                save(body)
                dve.wait_ge(*mid_pow_out.at(body, 1))
                normed(u, powout[:, 0:4]).then_inc(mid_u_ready.sem, 1)
                dve.wait_ge(*mid_u_ready.at(body, 1))
                for t in range(NT):
                    ins = V_.tensor_tensor_reduce(square[:, t, :], u[:, t, 0:D], u[:, t, 0:D], 1.0, 0.0,
                                                  ALU.mult, ALU.add, powin[:, t:t + 1])
                ins.then_inc(mid_pow_in.sem, 1)
                dve.wait_ge(*mid_pow_out.at(body, 2))
                V_.tensor_scalar(rnorm[:, :], powout[:, 0:4], RECIP_CAP, None, ALU.min).then_inc(rnorm_ready.sem, 1)

            def norm_products(body):
                dve.wait_ge(*rnorm_ready.at(body, 1))
                dve.wait_ge(*read_out(body, "RROW"))
                for t in range(NT):
                    ins = V_.tensor_scalar(sim[t], rrow[:, :], rnorm[:, t:t + 1], 1.0 / COS_EPS, ALU.mult, ALU.min)
                then(body, ins)

            def similarity(body, t):
                i = bank_of(body, f"DOTS{t}")
                dve.wait_ge(*filled(body, f"DOTS{t}"))
                V_.tensor_tensor(sim[t], sim[t], W[i][:, :], ALU.mult).then_inc(w_free[i].sem, 1)

            def attended(body, a):
                i = bank_of(body, f"AV{a}")
                dve.wait_ge(*filled(body, f"AV{a}"))
                bank = W[i][:, 0:2 * (D + 1)].rearrange("p (i c) -> p i c", i=2)
                then(body, V_.reciprocal(recip_m[:, 2 * a:2 * a + 2], bank[:, :, D]))
                for k in range(2):
                    t = 2 * a + k
                    ins = V_.scalar_tensor_tensor(out=n[:, t, :], in0=bank[:, k, 0:D], scalar=recip_m[:, t:t + 1],
                                                  in1=u[:, t, 0:D], op0=ALU.mult, op1=ALU.add)
                ins.then_inc(w_free[i].sem, 1)
                if a == 1:
                    dve.wait_ge(*read_out(body, "AV0"))
                    dve.wait_ge(*read_out(body, "AV1"))
                    V_.tensor_tensor(x[:, :, :], x[:, :, :], n[:, :, :], ALU.add).then_inc(x_new.sem, 1)

            def run(body):
                counted.pop(body.kind, None)
                for what, k in EVENTS[body.kind]:
                    if what == "setup":
                        (setup_latent, setup_experts)[k]()
                    elif what == "save":
                        save(body)
                    elif what == "mid":
                        mid(body)
                    elif what == "front":
                        front(body)
                    elif what == "max":
                        row_max(body, k)
                    elif what == "nmax":
                        split_max(body)
                    elif what == "sum":
                        out_copy(body, k)
                    elif what == "norm2":
                        norm2(body)
                    elif what == "finish":
                        finish(body)
                    elif what != "work":
                        continue
                    elif k == "RROW":
                        norm_products(body)
                    elif k.startswith("DOTS"):
                        similarity(body, int(k[4:]))
                    elif k.startswith("AV"):
                        attended(body, int(k[2:]))
                    elif k == "LATENT":
                        latent(body)
                    elif k in ("Q", "QR", "K", "KR"):
                        rope(body, k)
                    elif k.startswith("T_OUT"):
                        divide(body, int(k[5:]))
                    elif k == "WO":
                        residual(body)
                    elif k == "LOGIT":
                        choose(body)
                    elif k.startswith("MASK"):
                        mask(body, int(k[4:]))
                assert counted.get(body.kind, 0) == DVE_STEPS[body.kind], counted

            V_.memset(high_bits[:, :], HIGH_BITS)
            V_.memset(kz[:, :, :, :], 0.0).then_inc(cleared, 1)
            bodies(dve, run)

def rope_tables():
    half = HD // 2
    inv_freq = (np.float32(1.0) / np.power(np.float32(10000.0), np.arange(half, dtype=np.float32) / np.float32(half)))
    angle = np.arange(T, dtype=np.float32)[None, :] * inv_freq.astype(np.float32)[:, None]
    rows = np.tile(np.repeat(angle.astype(np.float64), NH, axis=0), (2, 1))
    return np.cos(rows).astype(np.float32), np.sin(rows).astype(np.float32)


def kernel(**inputs):
    import numpy as _np
    import concourse.bacc as _bacc
    from concourse import mybir as _mybir
    from concourse.bass_utils import run_bass_kernel_spmd as _run

    g = {k: _np.asarray(a) for k, a in inputs.items()}
    f = lambda name: g["L0_ffn_" + name]
    by_dim = lambda m: m.reshape(m.shape[0], NPAIR, 2, HD).transpose(0, 3, 2, 1).reshape(m.shape)
    cos, sin = rope_tables()
    arrays = {
        "x": g["L0_attn_x"],
        "WqT": by_dim(f("Wq").T), "WdkvT": f("Wdkv").T, "WukT": by_dim(f("Wuk").T), "WuvT": f("Wuv").T, "WoT": f("Wo").T,
        "gateT": f("gate_w").T, "gate_b": f("gate_b").reshape(1, NE),
        "b1T": f("b1").reshape(NCH, P).T, "b2": f("b2"),
        "n1": f("norm1_w").reshape(P, 1), "n2": f("norm2_w").reshape(P, 1),
        "ln_g": f("ln_g").reshape(LAT, 1), "ln_b": f("ln_b").reshape(LAT, 1),
        "W1T": f("W1").reshape(NE * HID, D).T,
        "W2T": f("W2").transpose(0, 2, 1).reshape(NCH, P, D).transpose(1, 0, 2),
        "pad_q": _np.zeros((64 // HD - N_SLOT, P, T), _mybir.dt.np(BF16)),
        "pad_k": _np.repeat((_np.arange(64 - MAXROW) < 3).astype(_mybir.dt.np(BF16)), NH * T)
                    .reshape(64 // HD - N_SLOT, P, T),
        "cos": cos, "sin": sin,
    }
    nc = _bacc.Bacc("TRN2", target_bir_lowering=False, num_devices=1)
    arrays = {f"in_{k}": _np.ascontiguousarray(a) for k, a in arrays.items()}
    args = {k[3:]: nc.dram_tensor(k, a.shape, _mybir.dt.from_np(a.dtype), kind="ExternalInput").ap()
            for k, a in arrays.items()}
    out = nc.dram_tensor("out_0", (B, T, D), F32, kind="ExternalOutput").ap()
    program(nc, args.pop("x"), out, args)
    r = _run(nc, [arrays], core_ids=[0])
    return r.results[0]["out_0"]
```
